# Optimizing a Trainium2 kernel written in Bass

```python
import numpy as np
import jax
import jax.numpy as jnp

def _softmax(x, axis=-1):
    return jax.nn.softmax(x, axis=axis)

def _gelu(x):
    return jax.nn.gelu(x, approximate=True)

def _silu(x):
    return jax.nn.silu(x)

def _sigmoid(x):
    return jax.nn.sigmoid(x)

def _layernorm(x, axis=-1, eps=1e-05):
    m = jnp.mean(x, axis=axis, keepdims=True)
    v = jnp.var(x, axis=axis, keepdims=True)
    return (x - m) / jnp.sqrt(v + eps)

def _scatter_add(tgt, idx, src, axis=0):
    return tgt.at[idx].add(src)

def _segment_sum(src, seg, n):
    return jax.ops.segment_sum(src, seg, n)
kernel_name = 'mk_prb_d1_jaxref_r4_4b33e9'

def setup_inputs(seed: int=0):
    np.random.seed(seed)
    _w = jnp.asarray

    def _L0_attn_setup():
        import jax, jax.numpy as jnp
        import numpy as np
        GAMMA = 0.96875
        key = jax.random.key(seed)
        kx, kq, kk, kv = jax.random.split(key, 4)
        B, T, D = (4, 512, 256)
        x = jax.random.normal(kx, (B, T, D), dtype=jnp.float32)
        Wq = jax.random.normal(kq, (D, D), dtype=jnp.float32) * (1.0 / np.sqrt(D))
        Wk = jax.random.normal(kk, (D, D), dtype=jnp.float32) * (1.0 / np.sqrt(D))
        Wv = jax.random.normal(kv, (D, D), dtype=jnp.float32) * (1.0 / np.sqrt(D))
        return {'x': x, 'Wq': Wq, 'Wk': Wk, 'Wv': Wv}
    _L0_attn_in = _L0_attn_setup()

    def _L0_ffn_setup():
        import jax, jax.numpy as jnp
        import numpy as np
        B, S, H = (1, 512, 256)
        E, K = (16, 4)
        G, TG = (4, 2)
        I_MOE = 128
        N_SH = 2
        SCALE = 2.5

        def _mlp(x, gw, uw, dw):
            return jax.nn.silu(x @ gw.T) * (x @ uw.T) @ dw.T

        def _route(x2d, router_weight, e_bias):
            T = x2d.shape[0]
            scores = jax.nn.sigmoid(x2d @ router_weight.T)
            sc = scores + e_bias[None, :]
            group_scores = jnp.sum(jax.lax.top_k(sc.reshape(T, G, E // G), 2)[0], axis=-1)
            _, gidx = jax.lax.top_k(group_scores, TG)
            gmask = jnp.zeros((T, G), sc.dtype).at[jnp.arange(T)[:, None], gidx].set(1.0)
            smask = jnp.repeat(gmask, E // G, axis=1)
            masked = jnp.where(smask > 0, sc, 0.0)
            _, tidx = jax.lax.top_k(masked, K)
            tw = jnp.take_along_axis(scores, tidx, axis=1)
            tw = tw / (jnp.sum(tw, axis=-1, keepdims=True) + 1e-20)
            tw = tw * SCALE
            return (tidx, tw)

        def _moe_forward(hidden_states, router_weight, e_bias, gate_w, up_w, down_w, sh_gate_w, sh_up_w, sh_down_w):
            orig_shape = hidden_states.shape
            x = hidden_states.reshape(-1, H)
            T = x.shape[0]
            tidx, tw = _route(x, router_weight, e_bias)
            g = jnp.einsum('th,eih->tei', x, gate_w)
            u = jnp.einsum('th,eih->tei', x, up_w)
            h = jax.nn.silu(g) * u
            yo = jnp.einsum('tei,ehi->teh', h, down_w)
            combine = jnp.zeros((T, E), tw.dtype).at[jnp.arange(T)[:, None], tidx].add(tw)
            routed = jnp.einsum('te,teh->th', combine, yo)
            shared = _mlp(hidden_states.reshape(-1, H), sh_gate_w, sh_up_w, sh_down_w)
            return (routed + shared).reshape(orig_shape)
        key = jax.random.key(seed)
        ks = jax.random.split(key, 9)
        s = 0.02
        return {'hidden_states': jax.random.normal(ks[0], (B, S, H), jnp.float32), 'router_weight': jax.random.normal(ks[1], (E, H), jnp.float32) * s, 'e_bias': jnp.zeros((E,), jnp.float32), 'gate_w': jax.random.normal(ks[2], (E, I_MOE, H), jnp.float32) * s, 'up_w': jax.random.normal(ks[3], (E, I_MOE, H), jnp.float32) * s, 'down_w': jax.random.normal(ks[4], (E, H, I_MOE), jnp.float32) * s, 'sh_gate_w': jax.random.normal(ks[5], (N_SH * I_MOE, H), jnp.float32) * s, 'sh_up_w': jax.random.normal(ks[6], (N_SH * I_MOE, H), jnp.float32) * s, 'sh_down_w': jax.random.normal(ks[7], (H, N_SH * I_MOE), jnp.float32) * s}
    _L0_ffn_in = _L0_ffn_setup()
    _d = {'L0_attn_x': _L0_attn_in['x'], 'L0_attn_Wq': _L0_attn_in['Wq'], 'L0_attn_Wk': _L0_attn_in['Wk'], 'L0_attn_Wv': _L0_attn_in['Wv'], 'L0_ffn_router_weight': _L0_ffn_in['router_weight'], 'L0_ffn_e_bias': _L0_ffn_in['e_bias'], 'L0_ffn_gate_w': _L0_ffn_in['gate_w'], 'L0_ffn_up_w': _L0_ffn_in['up_w'], 'L0_ffn_down_w': _L0_ffn_in['down_w'], 'L0_ffn_sh_gate_w': _L0_ffn_in['sh_gate_w'], 'L0_ffn_sh_up_w': _L0_ffn_in['sh_up_w'], 'L0_ffn_sh_down_w': _L0_ffn_in['sh_down_w']}
    _x0 = _d['L0_attn_x']
    _d['L0_attn_x'] = jax.random.normal(jax.random.fold_in(jax.random.key(seed), 1), (4, 2048, 256), dtype=_x0.dtype)
    del _x0
    return _d

def reference(L0_attn_x, L0_attn_Wq, L0_attn_Wk, L0_attn_Wv, L0_ffn_router_weight, L0_ffn_e_bias, L0_ffn_gate_w, L0_ffn_up_w, L0_ffn_down_w, L0_ffn_sh_gate_w, L0_ffn_sh_up_w, L0_ffn_sh_down_w):

    def _L0_attn_ref(x, Wq, Wk, Wv):
        import jax, jax.numpy as jnp
        import numpy as np
        GAMMA = 0.96875
        B, T, _ = x.shape
        D = Wq.shape[1]
        Q = jnp.einsum('bti,id->btd', x, Wq)
        K = jnp.einsum('bti,id->btd', x, Wk)
        V = jnp.einsum('bti,id->btd', x, Wv)
        gamma = jnp.asarray(GAMMA, x.dtype)
        m = jnp.einsum('btd,bt->td', K, V.sum(axis=-1))

        def step(s, mt):
            s_new = gamma * s + mt
            return (s_new, s_new)
        _, states = jax.lax.scan(step, jnp.zeros((D,), x.dtype), m[1:])
        S = jnp.concatenate([states[:1], states], axis=0)
        S = S.reshape(-1, T).T
        return S[None, :, :] * Q

    def _L0_ffn_ref(hidden_states, router_weight, e_bias, gate_w, up_w, down_w, sh_gate_w, sh_up_w, sh_down_w):
        import jax, jax.numpy as jnp
        import numpy as np
        B, S, H = (1, 512, 256)
        E, K = (16, 4)
        G, TG = (4, 2)
        I_MOE = 128
        N_SH = 2
        SCALE = 2.5

        def _mlp(x, gw, uw, dw):
            return jax.nn.silu(x @ gw.T) * (x @ uw.T) @ dw.T

        def _route(x2d, router_weight, e_bias):
            T = x2d.shape[0]
            scores = jax.nn.sigmoid(x2d @ router_weight.T)
            sc = scores + e_bias[None, :]
            group_scores = jnp.sum(jax.lax.top_k(sc.reshape(T, G, E // G), 2)[0], axis=-1)
            _, gidx = jax.lax.top_k(group_scores, TG)
            gmask = jnp.zeros((T, G), sc.dtype).at[jnp.arange(T)[:, None], gidx].set(1.0)
            smask = jnp.repeat(gmask, E // G, axis=1)
            masked = jnp.where(smask > 0, sc, 0.0)
            _, tidx = jax.lax.top_k(masked, K)
            tw = jnp.take_along_axis(scores, tidx, axis=1)
            tw = tw / (jnp.sum(tw, axis=-1, keepdims=True) + 1e-20)
            tw = tw * SCALE
            return (tidx, tw)

        def _moe_forward(hidden_states, router_weight, e_bias, gate_w, up_w, down_w, sh_gate_w, sh_up_w, sh_down_w):
            orig_shape = hidden_states.shape
            x = hidden_states.reshape(-1, H)
            T = x.shape[0]
            tidx, tw = _route(x, router_weight, e_bias)
            g = jnp.einsum('th,eih->tei', x, gate_w)
            u = jnp.einsum('th,eih->tei', x, up_w)
            h = jax.nn.silu(g) * u
            yo = jnp.einsum('tei,ehi->teh', h, down_w)
            combine = jnp.zeros((T, E), tw.dtype).at[jnp.arange(T)[:, None], tidx].add(tw)
            routed = jnp.einsum('te,teh->th', combine, yo)
            shared = _mlp(hidden_states.reshape(-1, H), sh_gate_w, sh_up_w, sh_down_w)
            return (routed + shared).reshape(orig_shape)
        return _moe_forward(hidden_states, router_weight, e_bias, gate_w, up_w, down_w, sh_gate_w, sh_up_w, sh_down_w)
    x = L0_attn_x
    xn = _layernorm(x, axis=-1)
    x = x + _L0_attn_ref(xn, L0_attn_Wq, L0_attn_Wk, L0_attn_Wv) + _L0_ffn_ref(xn, L0_ffn_router_weight, L0_ffn_e_bias, L0_ffn_gate_w, L0_ffn_up_w, L0_ffn_down_w, L0_ffn_sh_gate_w, L0_ffn_sh_up_w, L0_ffn_sh_down_w)
    return x

_drawn_inputs = setup_inputs


def setup_inputs(seed=0):
    import zlib

    import numpy as np

    out = dict(_drawn_inputs(seed))
    spreads = {'L0_ffn_e_bias': (0.0, 0.8)}
    factors = {'L0_ffn_router_weight': 8.0,
     'L0_ffn_gate_w': 8.0,
     'L0_ffn_up_w': 8.0,
     'L0_ffn_down_w': 8.0,
     'L0_ffn_sh_gate_w': 8.0,
     'L0_ffn_sh_up_w': 8.0,
     'L0_ffn_sh_down_w': 8.0}
    for name, (base, spread) in spreads.items():
        noise = np.random.default_rng([zlib.crc32(name.encode()), seed]).standard_normal(out[name].shape)
        drawn = base * np.exp(spread * noise) if base else spread * noise
        out[name] = jnp.asarray(drawn.astype(out[name].dtype))
    for name, factor in factors.items():
        out[name] = (out[name] * factor).astype(out[name].dtype)
    return out
```

```python
from contextlib import ExitStack

import concourse.bass as bass
from concourse import mybir

ALU = mybir.AluOpType
ACT = mybir.ActivationFunctionType
AX_X = mybir.AxisListType.X
F32 = mybir.dt.float32
F32R = mybir.dt.float32r
BF16 = mybir.dt.bfloat16
I32 = mybir.dt.int32

P = 128
GAMMA = 0.96875
LN_EPS = 1e-5
TOP_GROUPS = 2
TOP_EXPERTS = 4
ROUTE_SCALE = 2.5


class Program:

    def __init__(self, new_semaphore):
        self.new_semaphore = new_semaphore
        self.sems = {}
        self.steps = {e: [] for e in ("sync", "scalar", "vector", "gpsimd", "tensor")}
        self.waited = {e: {} for e in self.steps}

    def sem(self, name):
        if name not in self.sems:
            self.sems[name] = [self.new_semaphore(name), 0]
        return self.sems[name]

    def wait(self, engine, *tokens):
        for name, value in [t for t in tokens if t is not None]:
            if self.waited[engine].get(name, 0) < value:
                self.waited[engine][name] = value
                handle = self.sem(name)[0]
                self.steps[engine].append(lambda e, handle=handle, value=value: e.wait_ge(handle, value))

    def do(self, engine, name, instruction, *tokens, by=1):
        self.wait(engine, *tokens)
        entry = self.sem(name)
        entry[1] += by
        self.steps[engine].append(lambda e, h=entry[0]: instruction(e).then_inc(h, by))
        return (name, entry[1])

    def more(self, engine, instruction, *tokens):
        self.wait(engine, *tokens)
        self.steps[engine].append(instruction)

    def dma(self, engine, slot, out, in_, *tokens):
        return self.do(engine, slot, lambda e: e.dma_start(out, in_), *tokens, by=16)

    def raw(self, engine, fn):
        self.steps[engine].append(fn)

    def run(self, engine, e):
        for step in self.steps[engine]:
            step(e)


def layer_kernel(nc, x, wq, wk, wv, router, bias, experts, out):
    B, T, D = x.shape
    KC = D // P
    NE = router.shape[1]
    F = P
    NU = experts.shape[0]
    NSH = NU - NE
    WN = experts.shape[2]
    GATE, UP, DOWN = 0, KC * F, 2 * KC * F
    NG = T // P
    GT = B * P
    RG = 4
    EG = 4
    EPG = NE // EG
    RT = RG * B
    RC = NE + 2
    SG = 2

    x_tiles = x.rearrange("b (g p) d -> g p b d", p=P)
    out_tiles = out.rearrange("b (g p) d -> g p b d", p=P)
    xt_dram = nc.dram_tensor("xn_transposed", [NG, P, KC * GT], F32, kind="Internal").ap()
    xs_dram = nc.dram_tensor("x_plus_shared", [NG, P, B * D], F32, kind="Internal").ap()

    with ExitStack() as ctx:
        def sb(name, shape, dt=F32):
            return ctx.enter_context(nc.sbuf_tensor(name, shape, dt))

        def bank(name, shape):
            return ctx.enter_context(nc.psum_tensor(name, shape, F32))

        w_hi = sb("w_hi", [P, NE * WN], F32R)
        w_lo = sb("w_lo", [P, NE * WN], F32R)
        w_raw = sb("w_raw", [P, WN])
        wq_hi = sb("wq_hi", [P, KC, D], F32R)
        wq_lo = sb("wq_lo", [P, KC, D], F32R)
        wk_hi = sb("wk_hi", [P, KC, D], F32R)
        wk_lo = sb("wk_lo", [P, KC, D], F32R)
        rw = sb("rw", [P, KC, RC])
        rw_hi = sb("rw_hi", [P, KC, RC], F32R)
        rw_lo = sb("rw_lo", [P, KC, RC], F32R)
        bias_all = sb("bias_all", [P, NE])
        ident = sb("ident", [P, P])
        ident16 = sb("ident16", [P, P], BF16)
        gamma_col = sb("gamma_col", [P, 1])
        minus_half = sb("minus_half", [P, B])
        earlier = sb("earlier", [P, EG, EG])
        restart = sb("restart", [P, RT, NE])
        pick = sb("pick", [3 * NE, NE], BF16)
        ones16 = sb("ones16", [P, 2], BF16)
        zeros16 = sb("zeros16", [1, 512], BF16)
        XR = 4
        xr = sb("xr", [P, XR, B, D])
        xn = sb("xn", [P, 2, B, D])
        stat = sb("stat", [P, B, 6])
        mean_var = sb("mean_var", [P, 2, B, 2])
        var_eps = sb("var_eps", [P, B])
        rstd = sb("rstd", [P, 2, B])
        xt = sb("xt", [P, 2, KC * GT])
        xh = sb("xh", [P, 2, KC * GT], F32R)
        xl = sb("xl", [P, 2, KC * GT], F32R)
        y = sb("y", [P, D])
        yh = sb("yh", [P, KC, SG * P], F32R)
        yl = sb("yl", [P, KC, SG * P], F32R)
        state = sb("state", [P, KC, T])
        gated = sb("gated", [P, GT])
        hid = sb("hid", [P, GT])
        hid_hi = sb("hid_hi", [P, GT], F32R)
        hid_lo = sb("hid_lo", [P, GT], F32R)
        logits = sb("logits", [P, RG, B * RC])
        score = sb("score", [P, RT, NE])
        biased = sb("biased", [P, RT, NE])
        pair_hi = sb("pair_hi", [P, RT * EG, 2])
        pair_lo = sb("pair_lo", [P, RT * EG, 2])
        g_a = sb("g_a", [P, RT * EG])
        g_b = sb("g_b", [P, RT * EG])
        g_score = sb("g_score", [P, RT * EG])
        r_a = sb("r_a", [P, RT * NE])
        r_b = sb("r_b", [P, RT * NE])
        r_c = sb("r_c", [P, RT * NE])
        top8 = sb("top8", [P, RT, 8])
        t_a = sb("t_a", [P, RT])
        chosen = sb("chosen", [P, RT, NE])
        chosen16 = sb("chosen16", [P, RT * NE], BF16)
        combine16 = sb("combine16", [P, NG * B, 3 * NE], BF16)
        counts = sb("counts", [1, NG * NE], I32)
        ct = sb("ct", [3 * NE, 2, GT], BF16)
        sq = xn[:, 0, :, :]

        gate_ps = bank("gate_ps", [P, 512])
        up_ps = bank("up_ps", [P, 512])
        y_ps = bank("y_ps", [P, 2, 512])
        tq_ps = bank("tq_ps", [P, 2, 512])
        m_ps = bank("m_ps", [P, 512])
        r_ps = bank("r_ps", [P, 512])

        prog = Program(lambda name: ctx.enter_context(nc.semaphore(name)))
        do, more, dma, wait = prog.do, prog.more, prog.dma, prog.wait

        def flat(ap):
            return ap.rearrange("p a b -> p (a b)")

        def past(tokens, g):
            return tokens[g] if g >= 0 else None

        z = do("gpsimd", "c_pool", lambda e: e.memset(ident[:, :], 0.0))
        const = {}
        const["ident"] = do("gpsimd", "c_pool", lambda e: e.affine_select(
            out=ident[:, :], in_=ident[:, :], compare_op=ALU.not_equal, fill=1.0, base=0,
            pattern=[[-1, P]], channel_multiplier=1), z)
        do("gpsimd", "c_pool", lambda e: e.memset(minus_half[:, :], -0.5))
        do("gpsimd", "c_pool", lambda e: e.memset(gamma_col[:, :], GAMMA))
        z = do("gpsimd", "c_pool", lambda e: e.memset(pick[:, :], 0.0))
        for k in range(3):
            z = do("gpsimd", "c_pool", lambda e, k=k: e.affine_select(
                out=pick[:, :], in_=pick[:, :], compare_op=ALU.not_equal, fill=1.0, base=-k * NE,
                pattern=[[-1, NE]], channel_multiplier=1), z)
        z = do("gpsimd", "c_pool", lambda e: e.memset(earlier[:, :, :], 0.0))
        for i in range(1, EG):
            z = do("gpsimd", "c_pool", lambda e, i=i: e.memset(earlier[:, i, 0:i], 1.0), z)
        z = do("gpsimd", "c_pool", lambda e: e.memset(restart[:, :, :], 1.0))
        z = do("gpsimd", "c_pool", lambda e: e.memset(restart[:, :, 0:1], 0.0), z)
        do("gpsimd", "c_pool", lambda e: e.memset(ones16[:, :], 1.0))
        z = do("gpsimd", "c_pool", lambda e: e.memset(zeros16[:, :], 0.0))
        const["all"] = do("gpsimd", "c_pool", lambda e: e.tensor_copy(ident16[:, :], ident[:, :]),
                          const["ident"])

        def split(load, raw, slot, hi, lo, free=(), unpack=lambda a: a):
            landed = dma("sync", slot, unpack(raw), load, *free)
            h = do("scalar", "w_hi", lambda e: e.copy(hi, raw), landed, *free)
            l = do("gpsimd", "w_lo", lambda e: e.tensor_tensor(lo, raw, hi.bitcast(F32), ALU.subtract),
                   landed, h, *free)
            return [h, l]

        def unit_slot(u):
            return u if u < NE else NE - NSH + (u - NE)

        unit_ready = {}
        staging = flat(state[:, :, :])
        staged = [0]

        def stage(n):
            staged[0] += n
            return staging[:, staged[0] - n:staged[0]]

        def load_unit(u, raw, slot, free=()):
            s = unit_slot(u) * WN
            unit_ready[u] = split(experts[u], raw, slot, w_hi[:, s:s + WN], w_lo[:, s:s + WN], free)

        x_loaded, xn_done, t_done, xt_done, xh_done, xl_done, xt_stored = {}, {}, {}, {}, {}, {}, {}
        xs_added, xs_stored, lg_done, vs_done, y_done, yt_done = {}, {}, {}, {}, {}, {}
        yh_done, yl_done, scanned, routed, score_done = {}, {}, {}, {}, {}
        last = {}

        def A_load(g):
            x_loaded[g] = dma("sync", f"x{g % XR}", xr[:, g % XR, :, :], x_tiles[g], past(xs_stored, g - XR))

        def A_norm(g):
            s, r = g % XR, g % 2
            for b in range(B):
                bn = do("vector", "bn", lambda e, b=b: e.bn_stats(stat[:, b, :], xr[:, s, b, :]),
                        x_loaded[g], last.get("aggr"))
            for b in range(B):
                ag = do("vector", "bn", lambda e, b=b: e.bn_aggr(mean_var[:, r, b, :], stat[:, b, :]), bn,
                        past(xn_done, g - 2))
            last["aggr"] = ag
            ve = do("gpsimd", "rstd", lambda e: e.tensor_scalar(
                var_eps[:, :], mean_var[:, r, :, 1], LN_EPS, None, ALU.add), ag, last.get("rstd"))
            rs = do("gpsimd", "rstd", lambda e: e.tensor_tensor(
                rstd[:, r, :], var_eps[:, :], minus_half[:, :], ALU.pow), ve, const["all"],
                past(xn_done, g - 2))
            last["rstd"] = rs
            for b in range(B):
                xn_done[g] = do("vector", "xn", lambda e, b=b: e.tensor_scalar(
                    xn[:, r, b, :], xr[:, s, b, :], mean_var[:, r, b, 0:1], rstd[:, r, b:b + 1],
                    ALU.subtract, ALU.mult), rs, past(y_done, g - 2), past(t_done, g - 2))

        def A_transpose(g):
            r = g % 2
            wait("tensor", const["ident"], xn_done[g], past(xt_done, g - 1))
            for c in range(KC):
                for b in range(B):
                    f = lambda e, c=c, b=b: e.transpose(
                        tq_ps[:, c, b * P:(b + 1) * P], xn[:, r, b, c * P:(c + 1) * P], ident[:, :])
                    if (c, b) == (KC - 1, B - 1):
                        t_done[g] = do("tensor", "t", f)
                    else:
                        more("tensor", f)

        def A_keep(g):
            r = g % 2
            xt_done[g] = do("scalar", "xt", lambda e: e.copy(xt[:, r, :], flat(tq_ps[:, :, :])),
                            t_done[g], past(xt_stored, g - 2), past(xl_done, g - 2))
            xt_stored[g] = dma("sync", f"xts{r}", xt_dram[g], xt[:, r, :], xt_done[g])

        def A_split(g, free):
            r = g % 2
            xh_done[g] = do("scalar", "xh", lambda e: e.copy(xh[:, r, :], xt[:, r, :]), xt_done[g], *free)
            xl_done[g] = do("gpsimd", "xl", lambda e: e.tensor_tensor(
                xl[:, r, :], xt[:, r, :], xh[:, r, :].bitcast(F32), ALU.subtract), xh_done[g], *free)

        def parts(hi_l, lo_l, hi_r, lo_r):
            return ((hi_l, hi_r), (hi_l, lo_r), (lo_l, hi_r))

        def A_logits(g):
            r = g % 2
            wait("tensor", xh_done[g], xl_done[g], last.get("rps_read"), *router_ready)
            for b in range(B):
                for c in range(KC):
                    tok = slice(c * GT + b * P, c * GT + (b + 1) * P)
                    for k, (l, w) in enumerate(parts(xh[:, r, tok], xl[:, r, tok], rw_hi[:, c, :], rw_lo[:, c, :])):
                        f = lambda e, l=l, w=w, b=b, c=c, k=k: e.matmul(
                            r_ps[:, b * RC:(b + 1) * RC], l, w, start=(c == 0 and k == 0),
                            stop=(c == KC - 1 and k == 2))
                        if (b, c, k) == (B - 1, KC - 1, 2):
                            lg_done[g] = do("tensor", "lg", f)
                        else:
                            more("tensor", f)

        def A_logits_out(g):
            vs_done[g] = do("vector", "lgc", lambda e: e.tensor_copy(logits[:, g % RG, :], r_ps[:, 0:B * RC]),
                            lg_done[g], past(score_done, g // RG - 1))
            last["rps_read"] = vs_done[g]

        def A_values(g):
            r = g % 2
            v = lambda b: logits[:, g % RG, b * RC + NE:b * RC + NE + 1]
            t = do("vector", "y", lambda e: e.tensor_scalar(y[:, :], xn[:, r, 0, :], v(0), None, ALU.mult),
                   vs_done[g], past(yt_done, g - 1))
            for b in range(1, B):
                t = do("vector", "y", lambda e, b=b: e.scalar_tensor_tensor(
                    y[:, :], xn[:, r, b, :], v(b), y[:, :], ALU.mult, ALU.add), t)
            y_done[g] = t

        def A_y_transpose(g):
            wait("tensor", y_done[g], last.get("mps_read"))
            for c in range(KC):
                f = lambda e, c=c: e.transpose(m_ps[:, c * P:(c + 1) * P], y[:, c * P:(c + 1) * P], ident[:, :])
                if c == KC - 1:
                    yt_done[g] = do("tensor", "yt", f)
                else:
                    more("tensor", f)
            half = slice((g % SG) * P, (g % SG + 1) * P)
            ps = m_ps[:, 0:D].rearrange("p (c t) -> p c t", c=KC)
            yh_done[g] = do("scalar", "yh", lambda e: e.copy(yh[:, :, half], ps), yt_done[g], last.get("m"))
            yl_done[g] = do("vector", "yl", lambda e: e.tensor_tensor(
                yl[:, :, half], ps, yh[:, :, half].bitcast(F32), ALU.subtract), yh_done[g], last.get("m"))
            last["mps_read"] = yl_done[g]

        def A_scan(g):
            wait("tensor", yh_done[g], yl_done[g], *wk_ready)
            n = SG * P
            for c in range(KC):
                k = 0
                for i in range(KC):
                    col = slice(c * P, (c + 1) * P)
                    for l, w in parts(wk_hi[:, i, col], wk_lo[:, i, col], yh[:, i, :], yl[:, i, :]):
                        f = lambda e, l=l, w=w, c=c, k=k: e.matmul(
                            m_ps[:, c * n:(c + 1) * n], l, w, start=(k == 0), stop=(k == 3 * KC - 1))
                        k += 1
                        if (c, k) == (KC - 1, 3 * KC):
                            last["m"] = do("tensor", "m", f)
                        else:
                            more("tensor", f)
            t0 = (g - SG + 1) * P
            for c in range(KC):
                a = 1 if t0 == 0 else 0
                init = 0.0 if t0 == 0 else state[:, c, t0 - 1:t0]
                s = do("vector", "scan", lambda e, c=c, a=a, init=init: e.tensor_tensor_scan(
                    state[:, c, t0 + a:t0 + n], gamma_col[:, :].broadcast_to([P, n - a]), m_ps[:, c * n + a:(c + 1) * n], init,
                    ALU.mult, ALU.add), last["m"], last.get(f"scan{c}"), const["all"], *staging_free)
                last[f"scan{c}"] = s
            if t0 == 0:
                s = do("vector", "scan", lambda e: e.tensor_copy(state[:, :, 0:1], state[:, :, 1:2]), s)
            last["mps_read"] = last["scan"] = s

        def A_unit(q, s):
            r, w = q % 2, unit_slot(NE + s) * WN
            for name, ps, base, free in (("gate", gate_ps, GATE, last.get("silu")), ("up", up_ps, UP, last.get("hid"))):
                wait("tensor", xh_done[q], xl_done[q], free, *unit_ready[NE + s])
                k = 0
                for c in range(KC):
                    ws = slice(w + base + c * F, w + base + (c + 1) * F)
                    xs = slice(c * GT, (c + 1) * GT)
                    for l, m in parts(w_hi[:, ws], w_lo[:, ws], xh[:, r, xs], xl[:, r, xs]):
                        f = lambda e, l=l, m=m, k=k, ps=ps: e.matmul(ps[:, :], l, m, start=(k == 0), stop=(k == 3 * KC - 1))
                        k += 1
                        if k == 3 * KC:
                            last[name] = do("tensor", name, f)
                        else:
                            more("tensor", f)
            return dict(last)

        def A_hidden():
            prev_hid, prev_down = last.get("hid"), last.get("down")
            last["silu"] = do("scalar", "silu", lambda e: e.activation(gated[:, :], gate_ps[:, :], ACT.Silu),
                              last["gate"], prev_hid)
            last["hid"] = do("vector", "hid", lambda e: e.tensor_tensor(hid[:, :], gated[:, :], up_ps[:, :], ALU.mult),
                             last["silu"], last["up"], last.get("hh"), last.get("hl"))

        def A_hidden_split(prev_down):
            last["hh"] = do("scalar", "hh", lambda e: e.copy(hid_hi[:, :], hid[:, :]), last["hid"], prev_down)
            last["hl"] = do("gpsimd", "hl", lambda e: e.tensor_tensor(
                hid_lo[:, :], hid[:, :], hid_hi[:, :].bitcast(F32), ALU.subtract), last["hh"], prev_down)

        def down_products(e, w, first):
            for b in range(B):
                tok = slice(b * P, (b + 1) * P)
                col = slice(b % 2 * D, (b % 2 + 1) * D)
                for k, (l, m) in enumerate(parts(hid_hi[:, tok], hid_lo[:, tok], w_hi[:, w], w_lo[:, w])):
                    ins = e.matmul(y_ps[:, b // 2, col], l, m, start=(first and b % 2 == 0 and k == 0),
                                   stop=(k == 2), skip_group_check=True)
            return ins

        def A_down(q, s):
            w = unit_slot(NE + s) * WN + DOWN
            last["down"] = do("tensor", "down", lambda e: down_products(e, slice(w, w + D), s == 0),
                              last["hh"], last["hl"], last.get("y_read"))

        def A_add_shared(q):
            xs_added[q] = do("vector", "xs", lambda e: e.tensor_tensor(
                xr[:, q % XR, :, :].rearrange("p b d -> p (b d)"),
                xr[:, q % XR, :, :].rearrange("p b d -> p (b d)"), flat(y_ps[:, :, :]), ALU.add),
                last["down"], xn_done[q])
            last["y_read"] = xs_added[q]
            xs_stored[q] = dma("sync", f"xss{q % XR}", xs_dram[q], flat(xr[:, q % XR, :, :]), xs_added[q])

        def A_route(n):
            cols = RT * NE
            lg = logits[:, :, :].rearrange("p g (b r) -> p (g b) r", r=RC)[:, :, 0:NE]
            score_done[n] = do("scalar", "score", lambda e: e.activation(score[:, :, :], lg, ACT.Sigmoid),
                               vs_done[RG * n + RG - 1], last.get("routed"))
            t = score_done[n]

            def v(f, *tokens):
                return do("vector", "route", f, *tokens)

            sc, sb3 = flat(score[:, :, :]), biased[:, :, :]
            t = v(lambda e: e.tensor_tensor(sb3, score[:, :, :], bias_all[:, :].unsqueeze(1).broadcast_to([P, RT, NE]), ALU.add),
                  t, last.get("routed"), bias_ready)
            pairs = biased[:, :, :].rearrange("p t (h k) -> p (t h) k", k=2)
            ph, pl = flat(pair_hi[:, :, :]), flat(pair_lo[:, :, :])
            v(lambda e: e.tensor_tensor(ph, pairs[:, :, 0], pairs[:, :, 1], ALU.max), t)
            t = v(lambda e: e.tensor_tensor(pl, pairs[:, :, 0], pairs[:, :, 1], ALU.min))
            v(lambda e: e.tensor_tensor(g_a[:, :], pair_hi[:, :, 0], pair_hi[:, :, 1], ALU.min), t)
            t = v(lambda e: e.tensor_tensor(g_b[:, :], pair_lo[:, :, 0], pair_lo[:, :, 1], ALU.max))
            t = v(lambda e: e.tensor_tensor(g_a[:, :], g_a[:, :], g_b[:, :], ALU.max), t)
            t = v(lambda e: e.tensor_tensor(g_b[:, :], pair_hi[:, :, 0], pair_hi[:, :, 1], ALU.max), t)
            t = v(lambda e: e.tensor_tensor(g_score[:, :], g_a[:, :], g_b[:, :], ALU.add), t)
            gj = g_score[:, :].rearrange("p (t j) -> p t j", j=EG).unsqueeze(2).broadcast_to([P, RT, EG, EG])
            gi = g_score[:, :].rearrange("p (t i) -> p t i", i=EG).unsqueeze(3).broadcast_to([P, RT, EG, EG])
            ra4 = r_a[:, 0:RT * EG * EG].rearrange("p (t i j) -> p t i j", i=EG, j=EG)
            rb4 = r_b[:, 0:RT * EG * EG].rearrange("p (t i j) -> p t i j", i=EG, j=EG)
            v(lambda e: e.tensor_tensor(ra4, gj, gi, ALU.is_ge), t)
            t = v(lambda e: e.tensor_tensor(rb4, gj, gi, ALU.is_gt))
            t = v(lambda e: e.tensor_tensor(ra4, ra4, earlier[:, :, :].unsqueeze(1).broadcast_to([P, RT, EG, EG]), ALU.mult), t, const["all"])
            t = v(lambda e: e.tensor_tensor(r_a[:, :], r_a[:, :], r_b[:, :], ALU.max), t)
            t = v(lambda e: e.tensor_reduce(g_a[:, :], r_a[:, :].rearrange("p (t j) -> p t j", j=EG), AX_X, ALU.add), t)
            t = v(lambda e: e.tensor_scalar(g_a[:, :], g_a[:, :], float(TOP_GROUPS), None, ALU.is_lt), t)
            masked = r_c[:, :].rearrange("p (t k) -> p t k", k=NE)
            t = v(lambda e: e.tensor_tensor(
                r_c[:, :].rearrange("p (h k) -> p h k", k=EPG), biased[:, :, :].rearrange("p t (h k) -> p (t h) k", k=EPG),
                g_a[:, :].unsqueeze(2).broadcast_to([P, RT * EG, EPG]), ALU.mult), t)
            for i in range(RT):
                t8 = v(lambda e, i=i: e.max(top8[:, i, :], masked[:, i, :]), t)
            fourth = top8[:, :, TOP_EXPERTS - 1:TOP_EXPERTS].broadcast_to([P, RT, NE])
            a3 = r_a[:, :].rearrange("p (t k) -> p t k", k=NE)
            b3 = r_b[:, :].rearrange("p (t k) -> p t k", k=NE)
            v(lambda e: e.tensor_tensor(a3, masked, fourth, ALU.is_gt), t8)
            t = v(lambda e: e.tensor_tensor(b3, masked, fourth, ALU.is_equal))
            v(lambda e: e.tensor_reduce(t_a[:, :], a3, AX_X, ALU.add), t)
            t = v(lambda e: e.tensor_tensor_scan(r_c[:, :], flat(restart[:, :, :]), r_b[:, :], 0.0, ALU.mult, ALU.add), t)
            t = v(lambda e: e.tensor_tensor(masked, masked, t_a[:, :].unsqueeze(2).broadcast_to([P, RT, NE]), ALU.add), t)
            t = v(lambda e: e.scalar_tensor_tensor(r_c[:, :], r_c[:, :], float(TOP_EXPERTS), r_b[:, :], ALU.is_le, ALU.mult), t)
            t = v(lambda e: e.tensor_tensor(flat(chosen[:, :, :]), r_a[:, :], r_c[:, :], ALU.add), t)
            v(lambda e: e.tensor_copy(chosen16[:, :], flat(chosen[:, :, :])), t, last.get("count"))
            t = v(lambda e: e.tensor_tensor(r_a[:, :], sc, flat(chosen[:, :, :]), ALU.mult))
            last["chosen16"] = t
            t = v(lambda e: e.tensor_reduce(t_a[:, :], a3, AX_X, ALU.add), t)
            t = v(lambda e: e.tensor_scalar(t_a[:, :], t_a[:, :], 1e-20, None, ALU.add), t)
            t = v(lambda e: e.reciprocal(t_a[:, :], t_a[:, :]), t)
            t = v(lambda e: e.scalar_tensor_tensor(a3, a3, ROUTE_SCALE, t_a[:, :].unsqueeze(2).broadcast_to([P, RT, NE]), ALU.mult, ALU.mult), t)
            part = lambda k: combine16[:, n * RT:(n + 1) * RT, k * NE:(k + 1) * NE]
            t = v(lambda e: e.tensor_copy(part(0), a3), t)
            t = v(lambda e: e.tensor_tensor(a3, a3, part(0), ALU.subtract), t)
            t = v(lambda e: e.tensor_copy(part(1), a3), t)
            t = v(lambda e: e.tensor_tensor(part(2), a3, part(1), ALU.subtract), t)
            last["routed"] = t
            count = r_ps[0:1, 0:cols]
            last["count"] = do("tensor", "count", lambda e: e.matmul(count, ones16[:, 0:1], chosen16[:, :], start=True, stop=True),
                               last["chosen16"], last.get("rps_read"), const["all"])
            t = v(lambda e: e.tensor_reduce(
                r_b[0:1, 0:RG * NE].rearrange("p (g k) -> p g k", k=NE),
                count.rearrange("p (g b k) -> p g k b", b=B, k=NE), AX_X, ALU.add), last["count"], t)
            last["rps_read"] = t
            t = v(lambda e: e.tensor_copy(counts[0:1, n * RG * NE:(n + 1) * RG * NE], r_b[0:1, 0:RG * NE]), t)
            last["routed"] = t

        A_load(0)
        rows = lambda w: w.rearrange("(c p) n -> p c n", p=P)
        rw_loaded = dma("sync", "rw", rw[:, :, 0:NE], rows(router))
        bias_ready = dma("sync", "bias", bias_all[:, :], bias.unsqueeze(0).broadcast_to([P, NE]))
        chunks = lambda a: a.rearrange("p (c n) -> p c n", c=KC)
        wv_raw = stage(KC * D)
        wv_loaded = dma("sync", "wv", chunks(wv_raw), rows(wv))
        rz = do("vector", "rwz", lambda e: e.memset(rw[:, :, NE + 1:RC], 0.0))
        rs = do("vector", "rwz", lambda e: e.tensor_reduce(rw[:, :, NE:NE + 1], chunks(wv_raw), AX_X, ALU.add), wv_loaded)
        rh = do("scalar", "rwh", lambda e: e.copy(rw_hi[:, :, :], rw[:, :, :]), rw_loaded, rs)
        rl = do("gpsimd", "rwl", lambda e: e.tensor_tensor(rw_lo[:, :, :], rw[:, :, :], rw_hi[:, :, :].bitcast(F32), ALU.subtract), rw_loaded, rs, rh)
        router_ready = [rh, rl]
        A_norm(0)
        for u in range(NE, NU):
            load_unit(u, stage(WN), f"unit{u}")
        A_load(1)
        wk_ready = split(rows(wk), stage(KC * D), "wk", flat(wk_hi[:, :, :]), flat(wk_lo[:, :, :]), unpack=chunks)
        wq_ready = split(rows(wq), stage(KC * D), "wq", flat(wq_hi[:, :, :]), flat(wq_lo[:, :, :]), unpack=chunks)
        staging_free = [rs] + unit_ready[NE] + unit_ready[NU - 1] + wk_ready + wq_ready

        units_done = {}
        for g in range(NG + 2):
            if g < NG:
                A_transpose(g)
                A_keep(g)
            if g + 1 < NG:
                A_norm(g + 1)
            q = g - 1
            if 0 <= q < NG:
                A_unit(q, 0)
                before = last.get("down")
                A_hidden()
            if g < NG:
                A_split(g, [past(units_done, g - 2), past(lg_done, g - 2)])
            if q >= 1 and q - 1 < NG:
                A_down(q - 1, 1)
                A_add_shared(q - 1)
            if g + 2 < NG:
                A_load(g + 2)
            if 0 <= q < NG:
                A_hidden_split(last.get("down"))
                A_y_transpose(q)
                if q % SG == SG - 1:
                    A_scan(q)
                A_unit(q, 1)
                units_done[q] = last["up"]
                A_hidden()
                A_down(q, 0)
                A_hidden_split(last["down"])
            if g < NG:
                A_logits(g)
                A_logits_out(g)
                A_values(g)
                if g % RG == RG - 1:
                    A_route(g // RG)
            if g < NE - NSH:
                load_unit(g, w_raw[:, :], "w_raw", unit_ready.get(g - 1, ()))
        for u in range(NE - NSH, NE):
            load_unit(u, w_raw[:, :], "w_raw", unit_ready[u - 1] + [last["down"]])

        wait("tensor", last["silu"], last["hid"], last["y_read"], last["mps_read"], last["rps_read"],
             xt_done[NG - 1], *wq_ready)
        for u in range(NE):
            wait("tensor", *unit_ready[u])
        wait("scalar", last["hid"], last["down"], last["hl"])
        wait("vector", last["hh"], last["hl"], last["scan"], y_done[NG - 1])
        wait("gpsimd", last["down"])
        for e in ("tensor", "scalar", "vector", "gpsimd"):
            wait(e, last["routed"])

        def new_sem(name):
            return ctx.enter_context(nc.semaphore(name))

        cb_s, gate_s, up_s, silu_s, comb_s, hid_s, hh_s, hl_s, down_s = (
            new_sem("u_" + n) for n in ("combine_ps", "gate", "up", "silu", "weighted", "hid", "hh", "hl", "down"))
        ENG = ("tensor", "scalar", "vector", "gpsimd")
        regs = {e: {} for e in ENG}
        raised_by = {"tensor": (cb_s, gate_s, up_s, down_s), "scalar": (silu_s, hh_s), "vector": (comb_s, hid_s),
                     "gpsimd": (hl_s,)}

        def start(name):
            def f(e):
                r = regs[name]
                r["count"] = [e.alloc_register(f"{name}_c{i}") for i in range(NE)]
                for k in ("done", "next") + (("prev", "have") if name == "tensor" else ()):
                    r[k] = e.alloc_register(f"{name}_{k}")
                e.reg_mov(r["done"], 1)
                e.reg_mov(r["next"], 2)
                for s in raised_by[name]:
                    e.sem_inc(s, 1)
            return f

        for n in ENG:
            prog.raw(n, start(n))

        def units(name, g, body, begin=None):
            def f(e):
                r = regs[name]
                if begin:
                    begin(e, r)
                e.load(r["count"], counts[0:1, g * NE:(g + 1) * NE])
                for u in range(NE):
                    with e.If(e.snap(r["count"][u]) > 0):
                        done, nxt = e.snap(r["done"]), e.snap(r["next"])
                        body(e, r, u, done, nxt)
                        e.reg_add(r["done"], r["done"], 1)
                        e.reg_add(r["next"], r["next"], 1)
            prog.raw(name, f)

        xt_loaded, xs_loaded, bh, bl, ct_ps, ct_done, q_done, flushed = {}, {}, {}, {}, {}, {}, {}, {}
        sq_done, sq_added, y_added, stored = {}, {}, {}, {}

        def B_load(g):
            xt_loaded[g] = dma("sync", f"bxt{g % 2}", xt[:, g % 2, :], xt_dram[g], xt_stored[g], past(bh, g - 2),
                               past(bl, g - 2), *([xt_stored[NG - 2 + g], xh_done[NG - 2 + g], xl_done[NG - 2 + g]] if g < 2 else []))
            xs_loaded[g] = dma("sync", f"bx{g % XR}", flat(xr[:, g % XR, :, :]), xs_dram[g], xs_stored[g],
                               past(stored, g - XR), xs_stored[NG - XR + g % XR], y_added.get(g - XR) if g >= XR else None)

        def B_split(g):
            free = [past(q_done, g - 1)] if g >= 2 else [last["up"], last["lg"]]
            bh[g] = do("scalar", "bxh", lambda e: e.copy(xh[:, g % 2, :], xt[:, g % 2, :]), xt_loaded[g], *free)
            bl[g] = do("gpsimd", "bxl", lambda e: e.tensor_tensor(
                xl[:, g % 2, :], xt[:, g % 2, :], xh[:, g % 2, :].bitcast(F32), ALU.subtract), bh[g], *free)

        def B_combine(g):
            wait("tensor", past(ct_done, g - 1))
            for b in range(B):
                f = lambda e, b=b: e.matmul(r_ps[0:3 * NE, b * P:(b + 1) * P], combine16[:, g * B + b, :],
                                            ident16[:, :], start=True, stop=True)
                if b == B - 1:
                    ct_ps[g] = do("tensor", "ctp", f)
                else:
                    more("tensor", f)
            ct_done[g] = do("scalar", "ct", lambda e: e.copy(ct[:, g % 2, :], r_ps[0:3 * NE, :]), ct_ps[g], past(q_done, g - 1))

        def B_query(g):
            wait("tensor", bh[g], bl[g], past(sq_done, g - 1))
            for b in range(B):
                for c in range(KC):
                    tok = slice(c * GT + b * P, c * GT + (b + 1) * P)
                    for k, (l, w) in enumerate(parts(xh[:, g % 2, tok], xl[:, g % 2, tok], wq_hi[:, c, :], wq_lo[:, c, :])):
                        f = lambda e, l=l, w=w, b=b, c=c, k=k: e.matmul(
                            tq_ps[:, b // 2, b % 2 * D:(b % 2 + 1) * D], l, w, start=(c == 0 and k == 0),
                            stop=(c == KC - 1 and k == 2))
                        if (b, c, k) == (B - 1, KC - 1, 2):
                            q_done[g] = do("tensor", "q", f)
                        else:
                            more("tensor", f)

        def B_attend(g):
            t0 = g * P
            s = state[:, (t0 % D) // P, t0 // D::T // D].unsqueeze(1).broadcast_to([P, B, D])
            q = flat(tq_ps[:, :, :]).rearrange("p (b d) -> p b d", b=B)
            sq_done[g] = do("vector", "sq", lambda e: e.tensor_tensor(sq, q, s, ALU.mult), q_done[g], past(sq_added, g - 1))
            xg = flat(xr[:, g % XR, :, :])
            sq_added[g] = do("gpsimd", "sqa", lambda e: e.tensor_tensor(xg, xg, flat(sq), ALU.add), sq_done[g], xs_loaded[g])

        def B_finish(g):
            xg = flat(xr[:, g % XR, :, :])
            y_added[g] = do("vector", "ya", lambda e: e.tensor_tensor(xg, xg, flat(y_ps[:, :, :]), ALU.add),
                            flushed[g], sq_added[g])
            stored[g] = dma("sync", f"out{g % XR}", out_tiles[g], xr[:, g % XR, :, :], y_added[g])

        def down_dynamic(e, r, done):
            e.wait_ge(hh_s, done)
            e.wait_ge(hl_s, done)
            at = e.snap(r["prev"], min_val=DOWN, max_val=(NE - 1) * WN + DOWN)
            down_products(e, bass.ds(at, D), False).then_inc(down_s, 1)

        def tensor_units(g):
            free = past(y_added, g - 1)

            def begin(e, r):
                e.reg_mov(r["have"], 0)
                e.reg_mov(r["prev"], DOWN)

            def body(e, r, u, done, nxt):
                w = u * WN
                e.wait_ge(comb_s, done)
                e.matmul(m_ps[:, :], pick[:, u:u + 1].broadcast_to([3 * NE, P]), ct[:, g % 2, :],
                         start=True, stop=True).then_inc(cb_s, 1)
                for ps, base, free_s, sem in ((gate_ps, GATE, silu_s, gate_s), (up_ps, UP, hid_s, up_s)):
                    e.wait_ge(free_s, done)
                    k = 0
                    for c in range(KC):
                        ws = slice(w + base + c * F, w + base + (c + 1) * F)
                        xs = slice(c * GT, (c + 1) * GT)
                        for l, m in parts(w_hi[:, ws], w_lo[:, ws], xh[:, g % 2, xs], xl[:, g % 2, xs]):
                            ins = e.matmul(ps[:, :], l, m, start=(k == 0), stop=(k == 3 * KC - 1))
                            k += 1
                    ins.then_inc(sem, 1)
                with e.If(e.snap(r["have"]) > 0):
                    down_dynamic(e, r, done)
                with e.Else():
                    if free:
                        e.wait_ge(prog.sem(free[0])[0], free[1])
                    for k in range(2):
                        e.matmul(y_ps[:, k, :], zeros16[:, 0:P], zeros16[:, :], start=True, stop=True,
                                 skip_group_check=True)
                e.reg_mov(r["have"], 1)
                e.reg_mov(r["prev"], w + DOWN)

            units("tensor", g, body, begin)

        def B_flush(g):
            def f(e):
                r = regs["tensor"]
                done = e.snap(r["done"])
                down_dynamic(e, r, done)
            prog.raw("tensor", f)
            flushed[g] = do("tensor", "flush", lambda e: e.matmul(
                y_ps[:, 1, D:D + P], zeros16[:, 0:P], zeros16[:, 0:P], start=False, stop=True, skip_group_check=True))

        def scalar_units(g):
            def body(e, r, u, done, nxt):
                e.wait_ge(gate_s, nxt)
                e.wait_ge(hid_s, done)
                e.activation(gated[:, :], gate_ps[:, :], ACT.Silu).then_inc(silu_s, 1)
                e.wait_ge(hid_s, nxt)
                e.wait_ge(down_s, done)
                e.copy(hid_hi[:, :], hid[:, :]).then_inc(hh_s, 1)
            units("scalar", g, body)

        def vector_units(g):
            def body(e, r, u, done, nxt):
                e.wait_ge(silu_s, nxt)
                e.wait_ge(cb_s, nxt)
                e.tensor_tensor(gated[:, :], gated[:, :], m_ps[:, :], ALU.mult).then_inc(comb_s, 1)
                e.wait_ge(comb_s, nxt)
                e.wait_ge(up_s, nxt)
                e.wait_ge(hh_s, done)
                e.wait_ge(hl_s, done)
                e.tensor_tensor(hid[:, :], gated[:, :], up_ps[:, :], ALU.mult).then_inc(hid_s, 1)
            units("vector", g, body)

        def pool_units(g):
            def body(e, r, u, done, nxt):
                e.wait_ge(hh_s, nxt)
                e.wait_ge(down_s, done)
                e.tensor_tensor(hid_lo[:, :], hid[:, :], hid_hi[:, :].bitcast(F32), ALU.subtract).then_inc(hl_s, 1)
            units("gpsimd", g, body)

        last["lg"] = lg_done[NG - 1]
        B_load(0)
        B_load(1)
        B_split(0)
        B_combine(0)
        B_query(0)
        for g in range(NG):
            wait("tensor", bh[g], bl[g], ct_done[g])
            B_attend(g)
            if g > 0:
                B_finish(g - 1)
            if g + 1 < NG:
                B_split(g + 1)
            if g + 2 < NG:
                B_load(g + 2)
            tensor_units(g)
            scalar_units(g)
            vector_units(g)
            pool_units(g)
            if g + 1 < NG:
                B_combine(g + 1)
                B_query(g + 1)
            B_flush(g)
        B_finish(NG - 1)
        wait("sync", *[stored[g] for g in range(NG - XR, NG)])

        block = ctx.enter_context(nc.Block())

        @block.sync
        def _(e):
            prog.run("sync", e)

        @block.scalar
        def _(e):
            prog.run("scalar", e)

        @block.vector
        def _(e):
            prog.run("vector", e)

        @block.gpsimd
        def _(e):
            prog.run("gpsimd", e)

        @block.tensor
        def _(e):
            prog.run("tensor", e)


def kernel(L0_attn_x, L0_attn_Wq, L0_attn_Wk, L0_attn_Wv, L0_ffn_router_weight, L0_ffn_e_bias, L0_ffn_gate_w,
           L0_ffn_up_w, L0_ffn_down_w, L0_ffn_sh_gate_w, L0_ffn_sh_up_w, L0_ffn_sh_down_w):
    import numpy as np
    import concourse.bacc as bacc
    from concourse.bass_utils import run_bass_kernel_spmd

    x = np.ascontiguousarray(L0_attn_x)
    D = x.shape[-1]
    E, F, _ = L0_ffn_gate_w.shape
    NSH = L0_ffn_sh_gate_w.shape[0] // F
    KC = D // P

    def inward(w):
        w = np.asarray(w)
        return w.reshape(w.shape[0], F, KC, P).transpose(0, 3, 2, 1).reshape(w.shape[0], P, KC * F)

    def outward(w):
        return np.asarray(w).transpose(0, 2, 1)

    gate = np.concatenate([inward(L0_ffn_gate_w), inward(np.asarray(L0_ffn_sh_gate_w).reshape(NSH, F, D))])
    up = np.concatenate([inward(L0_ffn_up_w), inward(np.asarray(L0_ffn_sh_up_w).reshape(NSH, F, D))])
    sh_down = np.asarray(L0_ffn_sh_down_w).reshape(D, NSH, F).transpose(1, 0, 2)
    down = np.concatenate([outward(L0_ffn_down_w), outward(sh_down)])
    arrays = {
        "x": x,
        "wq": np.ascontiguousarray(L0_attn_Wq),
        "wk": np.ascontiguousarray(L0_attn_Wk),
        "wv": np.ascontiguousarray(L0_attn_Wv),
        "router": np.ascontiguousarray(np.asarray(L0_ffn_router_weight).T),
        "bias": np.ascontiguousarray(L0_ffn_e_bias),
        "experts": np.ascontiguousarray(np.concatenate([gate, up, down], axis=2)),
    }
    nc = bacc.Bacc("TRN2", target_bir_lowering=False, num_devices=1)
    args = [nc.dram_tensor(n, a.shape, mybir.dt.from_np(a.dtype), kind="ExternalInput").ap() for n, a in arrays.items()]
    out = nc.dram_tensor("out", x.shape, F32, kind="ExternalOutput").ap()
    layer_kernel(nc, *args, out)
    r = run_bass_kernel_spmd(nc, [arrays], core_ids=[0])
    return r.results[0]["out"]
```

```python
from contextlib import ExitStack

import concourse.bass as bass
from concourse import mybir

ALU = mybir.AluOpType
ACT = mybir.ActivationFunctionType
AX_X = mybir.AxisListType.X
F32 = mybir.dt.float32
F32R = mybir.dt.float32r
BF16 = mybir.dt.bfloat16
I32 = mybir.dt.int32

P = 128
GAMMA = 0.96875
LN_EPS = 1e-5
TOP_GROUPS = 2
TOP_EXPERTS = 4
ROUTE_SCALE = 2.5


class Program:

    def __init__(self, new_semaphore):
        self.new_semaphore = new_semaphore
        self.sems = {}
        self.steps = {e: [] for e in ("sync", "scalar", "vector", "gpsimd", "tensor")}
        self.waited = {e: {} for e in self.steps}

    def sem(self, name):
        if name not in self.sems:
            self.sems[name] = [self.new_semaphore(name), 0]
        return self.sems[name]

    def wait(self, engine, *tokens):
        for name, value in [t for t in tokens if t is not None]:
            if self.waited[engine].get(name, 0) < value:
                self.waited[engine][name] = value
                handle = self.sem(name)[0]
                self.steps[engine].append(lambda e, handle=handle, value=value: e.wait_ge(handle, value))

    def do(self, engine, name, instruction, *tokens, by=1):
        self.wait(engine, *tokens)
        entry = self.sem(name)
        entry[1] += by
        self.steps[engine].append(lambda e, h=entry[0]: instruction(e).then_inc(h, by))
        return (name, entry[1])

    def more(self, engine, instruction, *tokens):
        self.wait(engine, *tokens)
        self.steps[engine].append(instruction)

    def dma(self, engine, slot, out, in_, *tokens):
        return self.do(engine, slot, lambda e: e.dma_start(out, in_), *tokens, by=16)

    def raw(self, engine, fn):
        self.steps[engine].append(fn)

    def run(self, engine, e):
        for step in self.steps[engine]:
            step(e)


def layer_kernel(nc, x, wq, wk, wv, router, bias, experts, out):
    B, T, D = x.shape
    KC = D // P
    NE = router.shape[1]
    F = P
    NU = experts.shape[0]
    NSH = NU - NE
    WN = experts.shape[2]
    GATE, UP, DOWN = 0, KC * F, 2 * KC * F
    NG = T // P
    GT = B * P
    RG = 4
    EG = 4
    EPG = NE // EG
    RT = RG * B
    RC = NE + 2
    SG = 2

    x_tiles = x.rearrange("b (g p) d -> g p b d", p=P)
    out_tiles = out.rearrange("b (g p) d -> g p b d", p=P)
    xt_dram = nc.dram_tensor("xn_transposed", [NG, P, KC * GT], F32, kind="Internal").ap()
    xs_dram = nc.dram_tensor("x_plus_shared", [NG, P, B * D], F32, kind="Internal").ap()

    with ExitStack() as ctx:
        def sb(name, shape, dt=F32):
            return ctx.enter_context(nc.sbuf_tensor(name, shape, dt))

        def bank(name, shape):
            return ctx.enter_context(nc.psum_tensor(name, shape, F32))

        w_hi = sb("w_hi", [P, NE * WN], F32R)
        w_lo = sb("w_lo", [P, NE * WN], F32R)
        w_raw = sb("w_raw", [P, WN])
        wq_hi = sb("wq_hi", [P, KC, D], F32R)
        wq_lo = sb("wq_lo", [P, KC, D], F32R)
        wk_hi = sb("wk_hi", [P, KC, D], F32R)
        wk_lo = sb("wk_lo", [P, KC, D], F32R)
        rw = sb("rw", [P, KC, RC])
        rw_parts = sb("rw_parts", [P, KC, 2 * RC], F32R)
        bias_all = sb("bias_all", [P, NE])
        ident = sb("ident", [P, P])
        ident16 = sb("ident16", [P, P], BF16)
        gamma_col = sb("gamma_col", [P, 1])
        minus_half = sb("minus_half", [P, B])
        earlier = sb("earlier", [P, EG, EG])
        restart = sb("restart", [P, RT, NE])
        pick = sb("pick", [3 * NE, NE], BF16)
        ones16 = sb("ones16", [P, 2], BF16)
        NZ = 32
        zeros16 = sb("zeros16", [1, P], BF16)
        XR = 4
        xr = sb("xr", [P, XR, B, D])
        xn = sb("xn", [P, 2, B, D])
        stat = sb("stat", [P, B, 6])
        mean_var = sb("mean_var", [P, 2, B, 2])
        var_eps = sb("var_eps", [P, B])
        rstd = sb("rstd", [P, 2, B])
        neg_mean = sb("neg_mean", [P, B])
        shift = sb("shift", [P, 2, B])
        xt = sb("xt", [P, 2, KC * GT])
        xh = sb("xh", [P, 2, KC * GT], F32R)
        xl = sb("xl", [P, 2, KC * GT], F32R)
        y = sb("y", [P, D])
        yh = sb("yh", [P, KC, SG * P], F32R)
        yl = sb("yl", [P, KC, SG * P], F32R)
        state = sb("state", [P, KC, T])
        gated = sb("gated", [P, GT])
        hid = sb("hid", [P, GT])
        hid_hi = sb("hid_hi", [P, GT], F32R)
        hid_lo = sb("hid_lo", [P, GT], F32R)
        logits = sb("logits", [P, RG, B * RC])
        score = sb("score", [P, RT, NE])
        biased = sb("biased", [P, RT, NE])
        pair_hi = sb("pair_hi", [P, RT * EG, 2])
        pair_lo = sb("pair_lo", [P, RT * EG, 2])
        g_a = sb("g_a", [P, RT * EG])
        g_b = sb("g_b", [P, RT * EG])
        g_score = sb("g_score", [P, RT * EG])
        r_a = sb("r_a", [P, RT * NE])
        r_b = sb("r_b", [P, RT * NE])
        r_c = sb("r_c", [P, RT * NE])
        top8 = sb("top8", [P, RT, 8])
        t_a = sb("t_a", [P, RT])
        chosen = sb("chosen", [P, RT, NE])
        chosen16 = sb("chosen16", [P, RT * NE], BF16)
        combine16 = sb("combine16", [P, NG * B, 3 * NE], BF16)
        counts = sb("counts", [1, NG * NE], I32)
        ct = sb("ct", [3 * NE, 2, GT], BF16)
        sq = xn[:, 0, :, :]

        gate_ps = bank("gate_ps", [P, 512])
        up_ps = bank("up_ps", [P, 512])
        y_ps = bank("y_ps", [P, 2, 512])
        tq_ps = bank("tq_ps", [P, 2, 512])
        m_ps = bank("m_ps", [P, 512])
        r_ps = bank("r_ps", [P, 512])

        prog = Program(lambda name: ctx.enter_context(nc.semaphore(name)))
        do, more, dma, wait = prog.do, prog.more, prog.dma, prog.wait

        def flat(ap):
            return ap.rearrange("p a b -> p (a b)")

        def past(tokens, g):
            return tokens[g] if g >= 0 else None

        z = do("gpsimd", "c_pool", lambda e: e.memset(ident[:, :], 0.0))
        const = {}
        const["ident"] = do("gpsimd", "c_pool", lambda e: e.affine_select(
            out=ident[:, :], in_=ident[:, :], compare_op=ALU.not_equal, fill=1.0, base=0,
            pattern=[[-1, P]], channel_multiplier=1), z)
        do("gpsimd", "c_pool", lambda e: e.memset(minus_half[:, :], -0.5))
        do("gpsimd", "c_pool", lambda e: e.memset(gamma_col[:, :], GAMMA))
        z = do("gpsimd", "c_pool", lambda e: e.memset(pick[:, :], 0.0))
        for k in range(3):
            z = do("gpsimd", "c_pool", lambda e, k=k: e.affine_select(
                out=pick[:, :], in_=pick[:, :], compare_op=ALU.not_equal, fill=1.0, base=-k * NE,
                pattern=[[-1, NE]], channel_multiplier=1), z)
        z = do("gpsimd", "c_pool", lambda e: e.memset(earlier[:, :, :], 0.0))
        for i in range(1, EG):
            z = do("gpsimd", "c_pool", lambda e, i=i: e.memset(earlier[:, i, 0:i], 1.0), z)
        z = do("gpsimd", "c_pool", lambda e: e.memset(restart[:, :, :], 1.0))
        z = do("gpsimd", "c_pool", lambda e: e.memset(restart[:, :, 0:1], 0.0), z)
        do("gpsimd", "c_pool", lambda e: e.memset(ones16[:, :], 1.0))
        z = do("gpsimd", "c_pool", lambda e: e.memset(zeros16[:, :], 0.0))
        const["all"] = do("gpsimd", "c_pool", lambda e: e.tensor_copy(ident16[:, :], ident[:, :]),
                          const["ident"])

        def split(landed, raw, hi, lo, free=(), engine="gpsimd"):
            h = do("scalar", "w_hi", lambda e: e.copy(hi, raw), landed, *free)
            l = do(engine, "w_lo_" + engine, lambda e: e.tensor_tensor(lo, raw, hi.bitcast(F32), ALU.subtract),
                   landed, h, *free)
            return [h, l]

        def unit_slot(u):
            return u if u < NE else NE - NSH + (u - NE)

        unit_ready = {}
        staging = flat(state[:, :, :])
        staged = [0]

        def stage(n):
            staged[0] += n
            return staging[:, staged[0] - n:staged[0]]

        def split_unit(u, landed, raw, free=(), engine="gpsimd"):
            s = unit_slot(u) * WN
            unit_ready[u] = split(landed, raw, w_hi[:, s:s + WN], w_lo[:, s:s + WN], free, engine)

        x_loaded, xn_done, t_done, xt_done, xh_done, xl_done, xt_stored = {}, {}, {}, {}, {}, {}, {}
        norm_ready = {}
        xs_added, xs_stored, lg_done, vs_done, y_done, yt_done = {}, {}, {}, {}, {}, {}
        yh_done, yl_done, scanned, routed, score_done = {}, {}, {}, {}, {}
        last = {}

        def A_load(g):
            x_loaded[g] = dma("sync", f"x{g % XR}", xr[:, g % XR, :, :], x_tiles[g], past(xs_stored, g - XR))

        def A_norm(g):
            s, r = g % XR, g % 2
            for b in range(B):
                bn = do("vector", "bn", lambda e, b=b: e.bn_stats(stat[:, b, :], xr[:, s, b, :]),
                        x_loaded[g], last.get("aggr"))
            for b in range(B):
                ag = do("vector", "bn", lambda e, b=b: e.bn_aggr(mean_var[:, r, b, :], stat[:, b, :]), bn,
                        past(norm_ready, g - 2))
            last["aggr"] = ag
            ve = do("gpsimd", "rstd", lambda e: e.tensor_scalar(
                var_eps[:, :], mean_var[:, r, :, 1], LN_EPS, None, ALU.add), ag, last.get("rstd"))
            do("gpsimd", "rstd", lambda e: e.tensor_scalar(neg_mean[:, :], mean_var[:, r, :, 0], -1.0, None, ALU.mult))
            rs = do("gpsimd", "rstd", lambda e: e.tensor_tensor(
                rstd[:, r, :], var_eps[:, :], minus_half[:, :], ALU.pow), ve, const["all"],
                past(xn_done, g - 2))
            last["rstd"] = norm_ready[g] = do("gpsimd", "rstd", lambda e: e.tensor_tensor(
                shift[:, r, :], neg_mean[:, :], rstd[:, r, :], ALU.mult), rs)

        def A_xn(g):
            s, r = g % XR, g % 2
            for b in range(B):
                xn_done[g] = do("scalar", "xn", lambda e, b=b: e.activation(
                    xn[:, r, b, :], xr[:, s, b, :], ACT.Identity, bias=shift[:, r, b:b + 1], scale=rstd[:, r, b:b + 1]),
                    norm_ready[g], past(y_done, g - 2), past(t_done, g - 2))

        def A_transpose(g):
            r = g % 2
            wait("tensor", const["ident"], xn_done[g], past(xt_done, g - 1))
            for c in range(KC):
                for b in range(B):
                    f = lambda e, c=c, b=b: e.transpose(
                        tq_ps[:, c, b * P:(b + 1) * P], xn[:, r, b, c * P:(c + 1) * P], ident[:, :])
                    if (c, b) == (KC - 1, B - 1):
                        t_done[g] = do("tensor", "t", f)
                    else:
                        more("tensor", f)

        def A_keep(g):
            r = g % 2
            xt_done[g] = do("scalar", "xt", lambda e: e.copy(xt[:, r, :], flat(tq_ps[:, :, :])),
                            t_done[g], past(xt_stored, g - 2), past(xl_done, g - 2))
            xt_stored[g] = dma("sync", f"xts{r}", xt_dram[g], xt[:, r, :], xt_done[g])

        def A_split(g, free):
            r = g % 2
            xh_done[g] = do("scalar", "xh", lambda e: e.copy(xh[:, r, :], xt[:, r, :]), xt_done[g], *free)
            xl_done[g] = do("gpsimd", "xl", lambda e: e.tensor_tensor(
                xl[:, r, :], xt[:, r, :], xh[:, r, :].bitcast(F32), ALU.subtract), xh_done[g], *free)

        def parts(hi_l, lo_l, hi_r, lo_r):
            return ((hi_l, hi_r), (hi_l, lo_r), (lo_l, hi_r))

        def A_logits(g):
            r = g % 2
            wait("tensor", xh_done[g], xl_done[g], last.get("rps_read"), *router_ready)
            for b in range(B):
                col = b * 2 * RC
                for c in range(KC):
                    tok = slice(c * GT + b * P, c * GT + (b + 1) * P)
                    more("tensor", lambda e, b=b, c=c, tok=tok, col=col: e.matmul(
                        r_ps[:, col:col + 2 * RC], xh[:, r, tok], rw_parts[:, c, :], start=(c == 0), stop=False,
                        skip_group_check=True))
                    f = lambda e, b=b, c=c, tok=tok, col=col: e.matmul(
                        r_ps[:, col:col + RC], xl[:, r, tok], rw_parts[:, c, 0:RC], start=False,
                        stop=(c == KC - 1), skip_group_check=True)
                    if (b, c) == (B - 1, KC - 1):
                        lg_done[g] = do("tensor", "lg", f)
                    else:
                        more("tensor", f)

        def A_logits_out(g):
            lg = logits[:, g % RG, :].rearrange("p (b r) -> p b r", r=RC)
            ps = r_ps[:, 0:B * 2 * RC].rearrange("p (b k r) -> p k b r", k=2, r=RC)
            hi = do("vector", "lgc", lambda e: e.tensor_copy(lg, ps[:, 0]),
                    lg_done[g], past(score_done, g // RG - 1))
            vs_done[g] = do("vector", "lgc", lambda e: e.tensor_tensor(lg, lg, ps[:, 1], ALU.add), hi)
            last["rps_read"] = vs_done[g]

        def A_values(g):
            r = g % 2
            v = lambda b: logits[:, g % RG, b * RC + NE:b * RC + NE + 1]
            t = do("vector", "y", lambda e: e.tensor_scalar(y[:, :], xn[:, r, 0, :], v(0), None, ALU.mult),
                   vs_done[g], past(yt_done, g - 1))
            for b in range(1, B):
                t = do("vector", "y", lambda e, b=b: e.scalar_tensor_tensor(
                    y[:, :], xn[:, r, b, :], v(b), y[:, :], ALU.mult, ALU.add), t)
            y_done[g] = t

        def A_y_transpose(g):
            wait("tensor", y_done[g], last.get("mps_read"))
            for c in range(KC):
                f = lambda e, c=c: e.transpose(m_ps[:, c * P:(c + 1) * P], y[:, c * P:(c + 1) * P], ident[:, :])
                if c == KC - 1:
                    yt_done[g] = do("tensor", "yt", f)
                else:
                    more("tensor", f)

        def A_y_split(g):
            half = slice((g % SG) * P, (g % SG + 1) * P)
            ps = m_ps[:, 0:D].rearrange("p (c t) -> p c t", c=KC)
            yh_done[g] = do("scalar", "yh", lambda e: e.copy(yh[:, :, half], ps), yt_done[g], last.get("m"))
            yl_done[g] = do("vector", "yl", lambda e: e.tensor_tensor(
                yl[:, :, half], ps, yh[:, :, half].bitcast(F32), ALU.subtract), yh_done[g], last.get("m"))
            last["mps_read"] = yl_done[g]

        def A_scan(g):
            wait("tensor", yh_done[g], yl_done[g], *wk_ready)
            n = SG * P
            for c in range(KC):
                k = 0
                for i in range(KC):
                    col = slice(c * P, (c + 1) * P)
                    for l, w in parts(wk_hi[:, i, col], wk_lo[:, i, col], yh[:, i, :], yl[:, i, :]):
                        f = lambda e, l=l, w=w, c=c, k=k: e.matmul(
                            m_ps[:, c * n:(c + 1) * n], l, w, start=(k == 0), stop=(k == 3 * KC - 1))
                        k += 1
                        if (c, k) == (KC - 1, 3 * KC):
                            last["m"] = do("tensor", "m", f)
                        else:
                            more("tensor", f)
            t0 = (g - SG + 1) * P
            for c in range(KC):
                a = 1 if t0 == 0 else 0
                init = 0.0 if t0 == 0 else state[:, c, t0 - 1:t0]
                s = do("vector", "scan", lambda e, c=c, a=a, init=init: e.tensor_tensor_scan(
                    state[:, c, t0 + a:t0 + n], gamma_col[:, :].broadcast_to([P, n - a]), m_ps[:, c * n + a:(c + 1) * n], init,
                    ALU.mult, ALU.add), last["m"], last.get(f"scan{c}"), const["all"], *staging_free)
                last[f"scan{c}"] = s
            if t0 == 0:
                s = do("vector", "scan", lambda e: e.tensor_copy(state[:, :, 0:1], state[:, :, 1:2]), s)
            last["mps_read"] = last["scan"] = s

        def A_unit(q, s):
            r, w = q % 2, unit_slot(NE + s) * WN
            for name, ps, base, free in (("gate", gate_ps, GATE, last.get("silu")), ("up", up_ps, UP, last.get("hid"))):
                wait("tensor", xh_done[q], xl_done[q], free, *unit_ready[NE + s])
                k = 0
                for c in range(KC):
                    ws = slice(w + base + c * F, w + base + (c + 1) * F)
                    xs = slice(c * GT, (c + 1) * GT)
                    for l, m in parts(w_hi[:, ws], w_lo[:, ws], xh[:, r, xs], xl[:, r, xs]):
                        f = lambda e, l=l, m=m, k=k, ps=ps: e.matmul(ps[:, :], l, m, start=(k == 0), stop=(k == 3 * KC - 1))
                        k += 1
                        if k == 3 * KC:
                            last[name] = do("tensor", name, f)
                        else:
                            more("tensor", f)
            return dict(last)

        def A_hidden():
            prev_hid, prev_down = last.get("hid"), last.get("down")
            last["silu"] = do("scalar", "silu", lambda e: e.activation(gated[:, :], gate_ps[:, :], ACT.Silu),
                              last["gate"], prev_hid)
            last["hid"] = do("vector", "hid", lambda e: e.tensor_tensor(hid[:, :], gated[:, :], up_ps[:, :], ALU.mult),
                             last["silu"], last["up"], last.get("hh"), last.get("hl"))

        def A_hidden_split(prev_down):
            last["hh"] = do("scalar", "hh", lambda e: e.copy(hid_hi[:, :], hid[:, :]), last["hid"], prev_down)
            last["hl"] = do("gpsimd", "hl", lambda e: e.tensor_tensor(
                hid_lo[:, :], hid[:, :], hid_hi[:, :].bitcast(F32), ALU.subtract), last["hh"], prev_down)

        def down_products(e, w, first):
            for b in range(B):
                tok = slice(b * P, (b + 1) * P)
                col = slice(b % 2 * D, (b % 2 + 1) * D)
                for k, (l, m) in enumerate(parts(hid_hi[:, tok], hid_lo[:, tok], w_hi[:, w], w_lo[:, w])):
                    ins = e.matmul(y_ps[:, b // 2, col], l, m, start=(first and b % 2 == 0 and k == 0),
                                   stop=(k == 2), skip_group_check=True)
            return ins

        def A_down(q, s):
            w = unit_slot(NE + s) * WN + DOWN
            last["down"] = do("tensor", "down", lambda e: down_products(e, slice(w, w + D), s == 0),
                              last["hh"], last["hl"], last.get("y_read"))

        def A_add_shared(q):
            xs_added[q] = do("vector", "xs", lambda e: e.tensor_tensor(
                xr[:, q % XR, :, :].rearrange("p b d -> p (b d)"),
                xr[:, q % XR, :, :].rearrange("p b d -> p (b d)"), flat(y_ps[:, :, :]), ALU.add),
                last["down"], xn_done[q])
            last["y_read"] = xs_added[q]
            xs_stored[q] = dma("sync", f"xss{q % XR}", xs_dram[q], flat(xr[:, q % XR, :, :]), xs_added[q])

        def A_route(n):
            cols = RT * NE
            lg = logits[:, :, :].rearrange("p g (b r) -> p (g b) r", r=RC)[:, :, 0:NE]
            score_done[n] = do("scalar", "score", lambda e: e.activation(score[:, :, :], lg, ACT.Sigmoid),
                               vs_done[RG * n + RG - 1], last.get("routed"))
            t = score_done[n]
            yield

            def v(f, *tokens):
                return do("vector", "route", f, *tokens)

            sc, sb3 = flat(score[:, :, :]), biased[:, :, :]
            t = v(lambda e: e.tensor_tensor(sb3, score[:, :, :], bias_all[:, :].unsqueeze(1).broadcast_to([P, RT, NE]), ALU.add),
                  t, last.get("routed"), bias_ready)
            yield
            pairs = biased[:, :, :].rearrange("p t (h k) -> p (t h) k", k=2)
            ph, pl = flat(pair_hi[:, :, :]), flat(pair_lo[:, :, :])
            v(lambda e: e.tensor_tensor(ph, pairs[:, :, 0], pairs[:, :, 1], ALU.max), t)
            yield
            t = v(lambda e: e.tensor_tensor(pl, pairs[:, :, 0], pairs[:, :, 1], ALU.min))
            yield
            v(lambda e: e.tensor_tensor(g_a[:, :], pair_hi[:, :, 0], pair_hi[:, :, 1], ALU.min), t)
            yield
            t = v(lambda e: e.tensor_tensor(g_b[:, :], pair_lo[:, :, 0], pair_lo[:, :, 1], ALU.max))
            yield
            t = v(lambda e: e.tensor_tensor(g_a[:, :], g_a[:, :], g_b[:, :], ALU.max), t)
            yield
            t = v(lambda e: e.tensor_tensor(g_b[:, :], pair_hi[:, :, 0], pair_hi[:, :, 1], ALU.max), t)
            yield
            t = v(lambda e: e.tensor_tensor(g_score[:, :], g_a[:, :], g_b[:, :], ALU.add), t)
            yield
            gj = g_score[:, :].rearrange("p (t j) -> p t j", j=EG).unsqueeze(2).broadcast_to([P, RT, EG, EG])
            gi = g_score[:, :].rearrange("p (t i) -> p t i", i=EG).unsqueeze(3).broadcast_to([P, RT, EG, EG])
            ra4 = r_a[:, 0:RT * EG * EG].rearrange("p (t i j) -> p t i j", i=EG, j=EG)
            rb4 = r_b[:, 0:RT * EG * EG].rearrange("p (t i j) -> p t i j", i=EG, j=EG)
            v(lambda e: e.tensor_tensor(ra4, gj, gi, ALU.is_ge), t)
            yield
            t = v(lambda e: e.tensor_tensor(rb4, gj, gi, ALU.is_gt))
            yield
            t = v(lambda e: e.tensor_tensor(ra4, ra4, earlier[:, :, :].unsqueeze(1).broadcast_to([P, RT, EG, EG]), ALU.mult), t, const["all"])
            yield
            t = v(lambda e: e.tensor_tensor(r_a[:, :], r_a[:, :], r_b[:, :], ALU.max), t)
            yield
            t = v(lambda e: e.tensor_reduce(g_a[:, :], r_a[:, :].rearrange("p (t j) -> p t j", j=EG), AX_X, ALU.add), t)
            yield
            t = v(lambda e: e.tensor_scalar(g_a[:, :], g_a[:, :], float(TOP_GROUPS), None, ALU.is_lt), t)
            yield
            masked = r_c[:, :].rearrange("p (t k) -> p t k", k=NE)
            t = v(lambda e: e.tensor_tensor(
                r_c[:, :].rearrange("p (h k) -> p h k", k=EPG), biased[:, :, :].rearrange("p t (h k) -> p (t h) k", k=EPG),
                g_a[:, :].unsqueeze(2).broadcast_to([P, RT * EG, EPG]), ALU.mult), t)
            yield
            for i in range(RT):
                t8 = v(lambda e, i=i: e.max(top8[:, i, :], masked[:, i, :]), t)
                yield
            fourth = top8[:, :, TOP_EXPERTS - 1:TOP_EXPERTS].broadcast_to([P, RT, NE])
            a3 = r_a[:, :].rearrange("p (t k) -> p t k", k=NE)
            b3 = r_b[:, :].rearrange("p (t k) -> p t k", k=NE)
            v(lambda e: e.tensor_tensor(a3, masked, fourth, ALU.is_gt), t8)
            yield
            t = v(lambda e: e.tensor_tensor(b3, masked, fourth, ALU.is_equal))
            yield
            v(lambda e: e.tensor_reduce(t_a[:, :], a3, AX_X, ALU.add), t)
            yield
            t = v(lambda e: e.tensor_tensor_scan(r_c[:, :], flat(restart[:, :, :]), r_b[:, :], 0.0, ALU.mult, ALU.add), t)
            yield
            t = v(lambda e: e.tensor_tensor(masked, masked, t_a[:, :].unsqueeze(2).broadcast_to([P, RT, NE]), ALU.add), t)
            yield
            t = v(lambda e: e.scalar_tensor_tensor(r_c[:, :], r_c[:, :], float(TOP_EXPERTS), r_b[:, :], ALU.is_le, ALU.mult), t)
            yield
            t = v(lambda e: e.tensor_tensor(flat(chosen[:, :, :]), r_a[:, :], r_c[:, :], ALU.add), t)
            yield
            v(lambda e: e.tensor_copy(chosen16[:, :], flat(chosen[:, :, :])), t, last.get("count"))
            yield
            t = v(lambda e: e.tensor_tensor(r_a[:, :], sc, flat(chosen[:, :, :]), ALU.mult))
            yield
            last["chosen16"] = t
            t = v(lambda e: e.tensor_reduce(t_a[:, :], a3, AX_X, ALU.add), t)
            yield
            t = v(lambda e: e.tensor_scalar(t_a[:, :], t_a[:, :], 1e-20, None, ALU.add), t)
            yield
            t = v(lambda e: e.reciprocal(t_a[:, :], t_a[:, :]), t)
            yield
            t = v(lambda e: e.scalar_tensor_tensor(a3, a3, ROUTE_SCALE, t_a[:, :].unsqueeze(2).broadcast_to([P, RT, NE]), ALU.mult, ALU.mult), t)
            yield
            part = lambda k: combine16[:, n * RT:(n + 1) * RT, k * NE:(k + 1) * NE]
            t = v(lambda e: e.tensor_copy(part(0), a3), t)
            yield
            t = v(lambda e: e.tensor_tensor(a3, a3, part(0), ALU.subtract), t)
            yield
            t = v(lambda e: e.tensor_copy(part(1), a3), t)
            yield
            t = v(lambda e: e.tensor_tensor(part(2), a3, part(1), ALU.subtract), t)
            yield
            last["routed"] = t
            count = r_ps[0:1, 0:cols]
            last["count"] = do("tensor", "count", lambda e: e.matmul(count, ones16[:, 0:1], chosen16[:, :], start=True, stop=True),
                               last["chosen16"], last.get("rps_read"), const["all"])
            t = v(lambda e: e.tensor_reduce(
                r_b[0:1, 0:RG * NE].rearrange("p (g k) -> p g k", k=NE),
                count.rearrange("p (g b k) -> p g k b", b=B, k=NE), AX_X, ALU.add), last["count"], t)
            yield
            last["rps_read"] = t
            t = v(lambda e: e.tensor_copy(counts[0:1, n * RG * NE:(n + 1) * RG * NE], r_b[0:1, 0:RG * NE]), t)
            last["routed"] = routed[n] = t

        xt_loaded, xs_loaded, bh, bl, ct_ps, ct_done, q_done, flushed = {}, {}, {}, {}, {}, {}, {}, {}
        sq_done, sq_added, y_added, stored, cleared = {}, {}, {}, {}, {}

        def B_load(g):
            xt_loaded[g] = dma("sync", f"bxt{g % 2}", xt[:, g % 2, :], xt_dram[g], xt_stored[g], 
                               *([bh[g - 2], bl[g - 2]] if g >= 2 else
                                 [xt_stored[NG - 2 + g], xh_done[NG - 2 + g], xl_done[NG - 2 + g]]))
            xs_loaded[g] = dma("sync", f"bx{g % XR}", flat(xr[:, g % XR, :, :]), xs_dram[g], xs_stored[g],
                               *([stored[g - XR]] if g >= XR else [xs_stored[NG - XR + g]]),
                               *(unit_ready[NE - 1] if g == SPARE else []))

        def B_split(g):
            free = [q_done[g - 1]] if g >= 2 else [units_done[NG - 2 + g], lg_done[NG - 2 + g]]
            bh[g] = do("scalar", "bxh", lambda e: e.copy(xh[:, g % 2, :], xt[:, g % 2, :]), xt_loaded[g], *free)
            bl[g] = do("gpsimd", "bxl", lambda e: e.tensor_tensor(
                xl[:, g % 2, :], xt[:, g % 2, :], xh[:, g % 2, :].bitcast(F32), ALU.subtract), bh[g], *free)

        def B_combine(g):
            wait("tensor", last["rps_read"], routed[g // RG])
            for b in range(B):
                f = lambda e, b=b: e.matmul(r_ps[0:3 * NE, b * P:(b + 1) * P], combine16[:, g * B + b, :],
                                            ident16[:, :], start=True, stop=True)
                if b == B - 1:
                    ct_ps[g] = do("tensor", "ctp", f)
                else:
                    more("tensor", f)
            ct_done[g] = do("scalar", "ct", lambda e: e.copy(ct[:, g % 2, :], r_ps[0:3 * NE, :]), ct_ps[g], past(q_done, g - 1))
            last["rps_read"] = ct_done[g]

        def B_query(g):
            wait("tensor", bh[g], bl[g], sq_done[g - 1] if g > 0 else xt_done[NG - 1], *wq_ready)
            for b in range(B):
                for c in range(KC):
                    tok = slice(c * GT + b * P, c * GT + (b + 1) * P)
                    for k, (l, w) in enumerate(parts(xh[:, g % 2, tok], xl[:, g % 2, tok], wq_hi[:, c, :], wq_lo[:, c, :])):
                        f = lambda e, l=l, w=w, b=b, c=c, k=k: e.matmul(
                            tq_ps[:, b // 2, b % 2 * D:(b % 2 + 1) * D], l, w, start=(c == 0 and k == 0),
                            stop=(c == KC - 1 and k == 2))
                        if (b, c, k) == (B - 1, KC - 1, 2):
                            q_done[g] = do("tensor", "q", f)
                        else:
                            more("tensor", f)

        def new_sem(name):
            return ctx.enter_context(nc.semaphore(name))

        cb_s, gate_s, up_s, silu_s, comb_s, hid_s, hh_s, hl_s, down_s = (
            new_sem("u_" + n) for n in ("combine_ps", "gate", "up", "silu", "weighted", "hid", "hh", "hl", "down"))
        ENG = ("tensor", "scalar", "vector")
        regs = {e: {} for e in ENG}
        raised_by = {"tensor": (cb_s, gate_s, up_s, down_s), "scalar": (silu_s,), "vector": (comb_s, hh_s, hid_s, hl_s)}

        def start(name):
            def f(e):
                r = regs[name]
                r["count"] = [e.alloc_register(f"{name}_c{i}") for i in range(NE)]
                for k in ("done", "next") + (("prev", "have") if name == "tensor" else ()):
                    r[k] = e.alloc_register(f"{name}_{k}")
                e.reg_mov(r["done"], 1)
                e.reg_mov(r["next"], 2)
                if name == "tensor":
                    e.reg_mov(r["prev"], DOWN)
                for s in raised_by[name]:
                    e.sem_inc(s, 1)
            return f

        for n in ENG:
            prog.raw(n, start(n))

        A_load(0)
        rows = lambda w: w.rearrange("(c p) n -> p c n", p=P)
        rw_loaded = dma("sync", "rw", rw[:, :, 0:NE], rows(router))
        bias_ready = dma("sync", "bias", bias_all[:, :], bias.unsqueeze(0).broadcast_to([P, NE]))
        chunks = lambda a: a.rearrange("p (c n) -> p c n", c=KC)
        wv_raw = stage(KC * D)
        wv_loaded = dma("sync", "wv", chunks(wv_raw), rows(wv))
        shared_raw = [stage(WN) for _ in range(NSH)]
        shared_landed = [dma("sync", f"unit{i}", raw, experts[NE + i]) for i, raw in enumerate(shared_raw)]
        A_load(1)
        wk_raw, wq_raw = stage(KC * D), stage(KC * D)
        wk_landed = dma("sync", "wk", chunks(wk_raw), rows(wk))
        wq_landed = dma("sync", "wq", chunks(wq_raw), rows(wq))
        A_norm(0)
        rz = do("vector", "rwz", lambda e: e.memset(rw[:, :, NE + 1:RC], 0.0))
        rs = do("vector", "rwz", lambda e: e.tensor_reduce(rw[:, :, NE:NE + 1], chunks(wv_raw), AX_X, ALU.add), wv_loaded)
        rh = do("scalar", "rwh", lambda e: e.copy(rw_parts[:, :, 0:RC], rw[:, :, :]), rw_loaded, rs)
        A_xn(0)
        A_norm(1)
        rl = do("vector", "rwl", lambda e: e.tensor_tensor(
            rw_parts[:, :, RC:2 * RC], rw[:, :, :], rw_parts[:, :, 0:RC].bitcast(F32), ALU.subtract), rw_loaded, rs, rh)
        router_ready = [rh, rl]

        def split_first_weights():
            for i in range(NSH):
                split_unit(NE + i, shared_landed[i], shared_raw[i], engine="vector")
            k = split(wk_landed, wk_raw, flat(wk_hi[:, :, :]), flat(wk_lo[:, :, :]), engine="vector")
            q = split(wq_landed, wq_raw, flat(wq_hi[:, :, :]), flat(wq_lo[:, :, :]), engine="vector")
            return k, q

        early_units = NE - NSH
        SPARE = 2
        route_steps = []

        def route(steps):
            for _ in range(steps):
                if route_steps and next(route_steps[0], "end") == "end":
                    route_steps.pop()

        units_done, unit_landed = {}, {}
        for g in range(NG + 2):
            if g <= early_units:
                unit_landed[g] = dma("sync", "w_raw", w_raw[:, :], experts[g], *unit_ready.get(g - 1, ()))
            q = g - 1
            if g < NG:
                A_transpose(g)
                A_keep(g)
            if 0 <= q < NG:
                A_unit(q, 0)
            if g < NG:
                A_split(g, [past(units_done, g - 2), past(lg_done, g - 2)])
            elif g == NG:
                B_load(0)
                B_split(0)
            if g == 0:
                wk_ready, wq_ready = split_first_weights()
                staging_free = [rs] + unit_ready[NE] + unit_ready[NU - 1] + wk_ready + wq_ready
            elif g + 1 < NG:
                A_norm(g + 1)
            if 0 <= q < NG:
                A_hidden()
                A_y_transpose(q)
            prev_down = last.get("down")
            if 1 <= q <= NG:
                A_down(q - 1, 1)
            if 0 <= q < NG:
                A_y_split(q)
            if 1 <= q <= NG:
                A_add_shared(q - 1)
            if g + 2 < NG:
                A_load(g + 2)
            if 0 <= q < NG:
                A_hidden_split(last.get("down"))
                if q % SG == SG - 1:
                    A_scan(q)
            if g <= NG:
                route(6)
            if g < early_units:
                split_unit(g, unit_landed[g], w_raw[:, :])
            if 0 <= q < NG:
                A_unit(q, 1)
                units_done[q] = last["up"]
                A_hidden()
            if g + 1 < NG:
                A_xn(g + 1)
            if 0 <= q < NG:
                A_down(q, 0)
                A_hidden_split(last["down"])
            if g <= NG:
                route(9)
            if g < NG:
                A_logits(g)
                A_logits_out(g)
                A_values(g)
                if g % RG == RG - 1:
                    route(1000)
                    route_steps.append(A_route(g // RG))
            elif g == NG:
                B_combine(0)
                B_query(0)
        spare = flat(xr[:, SPARE, :, :])[:, 0:WN]
        last_landed = dma("sync", "w_last", spare, experts[NE - 1], xs_stored[NG - XR + SPARE])

        wait("tensor", last["silu"], last["hid"], last["y_read"], last["mps_read"])
        for u in range(early_units):
            wait("tensor", *unit_ready[u])
        wait("scalar", last["hid"], last["down"], last["hl"])
        wait("vector", last["hh"], last["hl"], last["down"], last["scan"], y_done[NG - 1], t_done[NG - 1])

        def begin_units(g):
            for name in ENG:
                wait(name, routed[g // RG])
                prog.raw(name, lambda e, r=regs[name]: e.load(r["count"], counts[0:1, g * NE:(g + 1) * NE]))
            prog.raw("tensor", lambda e: e.reg_mov(regs["tensor"]["have"], 0))

        def unit(g, u):
            for name, body in (("tensor", tensor_unit), ("scalar", scalar_unit), ("vector", vector_unit)):
                def f(e, r=regs[name], body=body):
                    with e.If_ne(r["count"][u], 0):
                        body(e, r, g, u, e.snap(r["done"]), e.snap(r["next"]))
                        e.reg_add(r["done"], r["done"], 1)
                        e.reg_add(r["next"], r["next"], 1)
                prog.raw(name, f)

        def B_attend(g):
            t0 = g * P
            s = state[:, (t0 % D) // P, t0 // D::T // D].unsqueeze(1).broadcast_to([P, B, D])
            q = flat(tq_ps[:, :, :]).rearrange("p (b d) -> p b d", b=B)
            sq_done[g] = do("vector", "sq", lambda e: e.tensor_tensor(sq, q, s, ALU.mult), q_done[g], past(sq_added, g - 1))
            xg = flat(xr[:, g % XR, :, :])
            sq_added[g] = do("gpsimd", "sqa", lambda e: e.tensor_tensor(xg, xg, flat(sq), ALU.add), sq_done[g], xs_loaded[g])

        def B_finish(g):
            xg = flat(xr[:, g % XR, :, :])
            y_added[g] = do("vector", "ya", lambda e: e.tensor_tensor(xg, xg, flat(y_ps[:, :, :]), ALU.add),
                            flushed[g], sq_added[g])
            stored[g] = dma("sync", f"out{g % XR}", out_tiles[g], xr[:, g % XR, :, :], y_added[g])

        def B_clear(g):
            cleared[g] = do("vector", "clear", lambda e: e.memset(flat(y_ps[:, :, :]), 0.0),
                            past(y_added, g - 1), last["y_read"])

        def down_dynamic(e, r, done, g):
            at = e.snap(r["prev"], min_val=DOWN, max_val=(NE - 1) * WN + DOWN)
            e.wait_ge(prog.sem(cleared[g][0])[0], cleared[g][1])
            e.wait_ge(hh_s, done)
            for hid_part, down_parts in ((hid_hi, (w_hi, w_lo)), (hid_lo, (w_hi,))):
                if hid_part is hid_lo:
                    e.wait_ge(hl_s, done)
                for b in range(B):
                    for w in down_parts:
                        ins = e.matmul(y_ps[:, b // 2, b % 2 * D:(b % 2 + 1) * D], hid_part[:, b * P:(b + 1) * P],
                                       w[:, bass.ds(at, D)], start=False, stop=True, skip_group_check=True)
            ins.then_inc(down_s, 1)

        def tensor_unit(e, r, g, u, done, nxt):
            if g == 0 and u >= early_units:
                for sem_name, value in unit_ready[u]:
                    e.wait_ge(prog.sem(sem_name)[0], value)
            w = u * WN
            def inward(ps, base, sem):
                k = 0
                for c in range(KC):
                    ws = slice(w + base + c * F, w + base + (c + 1) * F)
                    xs = slice(c * GT, (c + 1) * GT)
                    for l, m in parts(w_hi[:, ws], w_lo[:, ws], xh[:, g % 2, xs], xl[:, g % 2, xs]):
                        ins = e.matmul(ps[:, :], l, m, start=(k == 0), stop=(k == 3 * KC - 1))
                        k += 1
                ins.then_inc(sem, 1)

            e.wait_ge(silu_s, done)
            inward(gate_ps, GATE, gate_s)
            e.wait_ge(comb_s, done)
            e.matmul(m_ps[:, :], pick[:, u:u + 1].broadcast_to([3 * NE, P]), ct[:, g % 2, :],
                     start=True, stop=True).then_inc(cb_s, 1)
            with e.If_ne(r["have"], 0):
                down_dynamic(e, r, done, g)
            e.wait_ge(hid_s, done)
            inward(up_ps, UP, up_s)
            e.reg_mov(r["have"], 1)
            e.reg_mov(r["prev"], w + DOWN)

        def B_flush(g):
            def f(e):
                r = regs["tensor"]
                down_dynamic(e, r, e.snap(r["done"]), g)
            prog.raw("tensor", f)
            flushed[g] = do("tensor", "flush", lambda e: e.matmul(
                y_ps[:, 1, D:D + NZ], zeros16[:, 0:P], zeros16[:, 0:NZ], start=False, stop=True, skip_group_check=True))

        def scalar_unit(e, r, g, u, done, nxt):
            e.wait_ge(gate_s, nxt)
            e.wait_ge(hid_s, done)
            e.activation(gated[:, :], gate_ps[:, :], ACT.Silu).then_inc(silu_s, 1)

        def vector_unit(e, r, g, u, done, nxt):
            e.wait_ge(silu_s, nxt)
            e.wait_ge(cb_s, nxt)
            e.tensor_tensor(gated[:, :], gated[:, :], m_ps[:, :], ALU.mult).then_inc(comb_s, 1)
            e.wait_ge(comb_s, nxt)
            e.wait_ge(up_s, nxt)
            e.wait_ge(down_s, done)
            e.tensor_tensor(hid_hi[:, :], gated[:, :], up_ps[:, :], ALU.mult).then_inc(hh_s, 1)
            e.wait_ge(hl_s, done)
            e.tensor_tensor(hid[:, :], gated[:, :], up_ps[:, :], ALU.mult).then_inc(hid_s, 1)
            e.wait_ge(hh_s, nxt)
            e.wait_ge(hid_s, nxt)
            e.tensor_tensor(hid_lo[:, :], hid[:, :], hid_hi[:, :].bitcast(F32), ALU.subtract).then_inc(hl_s, 1)

        B_load(1)
        for g in range(NG):
            wait("tensor", bh[g], bl[g], ct_done[g])
            B_attend(g)
            if g > 0:
                B_finish(g - 1)
            B_clear(g)
            if g + 1 < NG:
                B_split(g + 1)
            begin_units(g)
            for u in range(NE):
                unit(g, u)
                if (g, u) == (0, 2):
                    split_unit(early_units, unit_landed[early_units], w_raw[:, :], [last["down"]])
                if (g, u) == (0, 5):
                    split_unit(NE - 1, last_landed, spare, [last["down"]])
                if g < RG:
                    route(1)
            if g + 2 < NG:
                B_load(g + 2)
            if g + 1 < NG:
                B_combine(g + 1)
                B_query(g + 1)
            B_flush(g)
        B_finish(NG - 1)
        wait("sync", *[stored[g] for g in range(NG - XR, NG)])

        block = ctx.enter_context(nc.Block())

        @block.sync
        def _(e):
            prog.run("sync", e)

        @block.scalar
        def _(e):
            prog.run("scalar", e)

        @block.vector
        def _(e):
            prog.run("vector", e)

        @block.gpsimd
        def _(e):
            prog.run("gpsimd", e)

        @block.tensor
        def _(e):
            prog.run("tensor", e)


def kernel(L0_attn_x, L0_attn_Wq, L0_attn_Wk, L0_attn_Wv, L0_ffn_router_weight, L0_ffn_e_bias, L0_ffn_gate_w,
           L0_ffn_up_w, L0_ffn_down_w, L0_ffn_sh_gate_w, L0_ffn_sh_up_w, L0_ffn_sh_down_w):
    import numpy as np
    import concourse.bacc as bacc
    from concourse.bass_utils import run_bass_kernel_spmd

    x = np.ascontiguousarray(L0_attn_x)
    D = x.shape[-1]
    E, F, _ = L0_ffn_gate_w.shape
    NSH = L0_ffn_sh_gate_w.shape[0] // F
    KC = D // P

    def inward(w):
        w = np.asarray(w)
        return w.reshape(w.shape[0], F, KC, P).transpose(0, 3, 2, 1).reshape(w.shape[0], P, KC * F)

    def outward(w):
        return np.asarray(w).transpose(0, 2, 1)

    gate = np.concatenate([inward(L0_ffn_gate_w), inward(np.asarray(L0_ffn_sh_gate_w).reshape(NSH, F, D))])
    up = np.concatenate([inward(L0_ffn_up_w), inward(np.asarray(L0_ffn_sh_up_w).reshape(NSH, F, D))])
    sh_down = np.asarray(L0_ffn_sh_down_w).reshape(D, NSH, F).transpose(1, 0, 2)
    down = np.concatenate([outward(L0_ffn_down_w), outward(sh_down)])
    arrays = {
        "x": x,
        "wq": np.ascontiguousarray(L0_attn_Wq),
        "wk": np.ascontiguousarray(L0_attn_Wk),
        "wv": np.ascontiguousarray(L0_attn_Wv),
        "router": np.ascontiguousarray(np.asarray(L0_ffn_router_weight).T),
        "bias": np.ascontiguousarray(L0_ffn_e_bias),
        "experts": np.ascontiguousarray(np.concatenate([gate, up, down], axis=2)),
    }
    nc = bacc.Bacc("TRN2", target_bir_lowering=False, num_devices=1)
    args = [nc.dram_tensor(n, a.shape, mybir.dt.from_np(a.dtype), kind="ExternalInput").ap() for n, a in arrays.items()]
    out = nc.dram_tensor("out", x.shape, F32, kind="ExternalOutput").ap()
    layer_kernel(nc, *args, out)
    r = run_bass_kernel_spmd(nc, [arrays], core_ids=[0])
    return r.results[0]["out"]
```

```python
from contextlib import ExitStack

import concourse.bass as bass
from concourse import mybir

ALU = mybir.AluOpType
ACT = mybir.ActivationFunctionType
AX_X = mybir.AxisListType.X
F32 = mybir.dt.float32
F32R = mybir.dt.float32r
BF16 = mybir.dt.bfloat16
I32 = mybir.dt.int32

P = 128
GAMMA = 0.96875
LN_EPS = 1e-5
TOP_GROUPS = 2
TOP_EXPERTS = 4
ROUTE_SCALE = 2.5


class Program:

    def __init__(self, new_semaphore):
        self.new_semaphore = new_semaphore
        self.sems = {}
        self.steps = {e: [] for e in ("sync", "scalar", "vector", "gpsimd", "tensor")}
        self.waited = {e: {} for e in self.steps}

    def sem(self, name):
        if name not in self.sems:
            self.sems[name] = [self.new_semaphore(name), 0]
        return self.sems[name]

    def wait(self, engine, *tokens):
        for name, value in [t for t in tokens if t is not None]:
            if self.waited[engine].get(name, 0) < value:
                self.waited[engine][name] = value
                handle = self.sem(name)[0]
                self.steps[engine].append(lambda e, handle=handle, value=value: e.wait_ge(handle, value))

    def do(self, engine, name, instruction, *tokens, by=1):
        self.wait(engine, *tokens)
        entry = self.sem(name)
        entry[1] += by
        self.steps[engine].append(lambda e, h=entry[0]: instruction(e).then_inc(h, by))
        return (name, entry[1])

    def more(self, engine, instruction, *tokens):
        self.wait(engine, *tokens)
        self.steps[engine].append(instruction)

    def dma(self, engine, slot, out, in_, *tokens):
        return self.do(engine, slot, lambda e: e.dma_start(out, in_), *tokens, by=16)

    def raw(self, engine, fn):
        self.steps[engine].append(fn)

    def run(self, engine, e):
        for step in self.steps[engine]:
            step(e)


def layer_kernel(nc, x, wq, wk, wv, router, bias, experts, out):
    B, T, D = x.shape
    KC = D // P
    NE = router.shape[1]
    F = P
    NU = experts.shape[0]
    NSH = NU - NE
    WN = experts.shape[2]
    GATE, UP, DOWN = 0, KC * F, 2 * KC * F
    NG = T // P
    GT = B * P
    RG = 4
    EG = 4
    EPG = NE // EG
    RT = RG * B
    RC = NE + 2
    SG = 2

    x_tiles = x.rearrange("b (g p) d -> g p b d", p=P)
    out_tiles = out.rearrange("b (g p) d -> g p b d", p=P)
    xt_dram = nc.dram_tensor("xn_transposed", [NG, P, KC * GT], F32, kind="Internal").ap()
    xs_dram = nc.dram_tensor("x_plus_shared", [NG, P, B * D], F32, kind="Internal").ap()

    with ExitStack() as ctx:
        def sb(name, shape, dt=F32):
            return ctx.enter_context(nc.sbuf_tensor(name, shape, dt))

        def bank(name, shape):
            return ctx.enter_context(nc.psum_tensor(name, shape, F32))

        w_hi = sb("w_hi", [P, NE * WN], F32R)
        w_lo = sb("w_lo", [P, NE * WN], F32R)
        w_raw = sb("w_raw", [P, WN])
        wq_hi = sb("wq_hi", [P, KC, D], F32R)
        wq_lo = sb("wq_lo", [P, KC, D], F32R)
        wk_hi = sb("wk_hi", [P, KC, D], F32R)
        wk_lo = sb("wk_lo", [P, KC, D], F32R)
        rw = sb("rw", [P, KC, RC])
        rw_parts = sb("rw_parts", [P, KC, 2 * RC], F32R)
        bias_all = sb("bias_all", [P, NE])
        ident = sb("ident", [P, P])
        ident16 = sb("ident16", [P, P], BF16)
        gamma_col = sb("gamma_col", [P, 1])
        minus_half = sb("minus_half", [P, B])
        earlier = sb("earlier", [P, EG, EG])
        restart = sb("restart", [P, RT, NE])
        pick = sb("pick", [3 * NE, NE], BF16)
        ones16 = sb("ones16", [P, 2], BF16)
        XR = 4
        xr = sb("xr", [P, XR, B, D])
        xn = sb("xn", [P, 2, B, D])
        stat = sb("stat", [P, B, 6])
        mean_var = sb("mean_var", [P, 2, B, 2])
        var_eps = sb("var_eps", [P, B])
        rstd = sb("rstd", [P, 2, B])
        neg_mean = sb("neg_mean", [P, B])
        shift = sb("shift", [P, 2, B])
        xt = sb("xt", [P, 2, KC * GT])
        xh = sb("xh", [P, 2, KC * GT], F32R)
        xl = sb("xl", [P, 2, KC * GT], F32R)
        y = sb("y", [P, D])
        yh = sb("yh", [P, KC, SG * P], F32R)
        yl = sb("yl", [P, KC, SG * P], F32R)
        state = sb("state", [P, KC, T])
        gated = sb("gated", [P, GT])
        hid = sb("hid", [P, GT])
        hid_hi = sb("hid_hi", [P, GT], F32R)
        hid_lo = sb("hid_lo", [P, GT], F32R)
        logits = sb("logits", [P, RG, B * RC])
        score = sb("score", [P, RT, NE])
        biased = sb("biased", [P, RT, NE])
        pair_hi = sb("pair_hi", [P, RT * EG, 2])
        pair_lo = sb("pair_lo", [P, RT * EG, 2])
        g_a = sb("g_a", [P, RT * EG])
        g_b = sb("g_b", [P, RT * EG])
        g_score = sb("g_score", [P, RT * EG])
        r_a = sb("r_a", [P, RT * NE])
        r_b = sb("r_b", [P, RT * NE])
        r_c = sb("r_c", [P, RT * NE])
        top8 = sb("top8", [P, RT, 8])
        t_a = sb("t_a", [P, RT])
        chosen = sb("chosen", [P, RT, NE])
        chosen16 = sb("chosen16", [P, RT * NE], BF16)
        combine16 = sb("combine16", [P, NG * B, 3 * NE], BF16)
        counts = sb("counts", [1, NG * NE], I32)
        ct = sb("ct", [3 * NE, 2, GT], BF16)
        sq = xn[:, 0, :, :]

        gate_ps = bank("gate_ps", [P, 512])
        up_ps = bank("up_ps", [P, 512])
        y_ps = bank("y_ps", [P, 2, 512])
        tq_ps = bank("tq_ps", [P, 2, 512])
        m_ps = bank("m_ps", [P, 512])
        r_ps = bank("r_ps", [P, 512])

        prog = Program(lambda name: ctx.enter_context(nc.semaphore(name)))
        do, more, dma, wait = prog.do, prog.more, prog.dma, prog.wait

        def flat(ap):
            return ap.rearrange("p a b -> p (a b)")

        def past(tokens, g):
            return tokens[g] if g >= 0 else None

        z = do("gpsimd", "constants", lambda e: e.memset(ident[:, :], 0.0))
        const = {}
        const["ident"] = do("gpsimd", "constants", lambda e: e.affine_select(
            out=ident[:, :], in_=ident[:, :], compare_op=ALU.not_equal, fill=1.0, base=0,
            pattern=[[-1, P]], channel_multiplier=1), z)
        do("gpsimd", "constants", lambda e: e.memset(minus_half[:, :], -0.5))
        do("gpsimd", "constants", lambda e: e.memset(gamma_col[:, :], GAMMA))
        z = do("gpsimd", "constants", lambda e: e.memset(pick[:, :], 0.0))
        for k in range(3):
            z = do("gpsimd", "constants", lambda e, k=k: e.affine_select(
                out=pick[:, :], in_=pick[:, :], compare_op=ALU.not_equal, fill=1.0, base=-k * NE,
                pattern=[[-1, NE]], channel_multiplier=1), z)
        z = do("gpsimd", "constants", lambda e: e.memset(earlier[:, :, :], 0.0))
        for i in range(1, EG):
            z = do("gpsimd", "constants", lambda e, i=i: e.memset(earlier[:, i, 0:i], 1.0), z)
        z = do("gpsimd", "constants", lambda e: e.memset(restart[:, :, :], 1.0))
        z = do("gpsimd", "constants", lambda e: e.memset(restart[:, :, 0:1], 0.0), z)
        const["all"] = do("gpsimd", "constants", lambda e: e.memset(ones16[:, :], 1.0))
        const["ident16"] = do("scalar", "ident16", lambda e: e.copy(ident16[:, :], ident[:, :]), const["ident"])

        def split(landed, raw, hi, lo, free=(), engine="gpsimd"):
            h = do("scalar", "w_hi", lambda e: e.copy(hi, raw), landed, *free)
            l = do(engine, "w_lo_" + engine, lambda e: e.tensor_tensor(lo, raw, hi.bitcast(F32), ALU.subtract),
                   landed, h, *free)
            return [h, l]

        def unit_slot(u):
            return u if u < NE else NE - NSH + (u - NE)

        unit_ready = {}
        staging = flat(state[:, :, :])
        staged = [0]

        def stage(n):
            staged[0] += n
            return staging[:, staged[0] - n:staged[0]]

        def split_unit(u, landed, raw, free=(), engine="gpsimd"):
            s = unit_slot(u) * WN
            unit_ready[u] = split(landed, raw, w_hi[:, s:s + WN], w_lo[:, s:s + WN], free, engine)

        x_loaded, xn_done, t_done, xt_done, xh_done, xl_done, xt_stored = {}, {}, {}, {}, {}, {}, {}
        moments, norm_ready, xn_batch = {}, {}, {}
        xs_added, xs_stored, lg_done, vs_done, y_done, yt_done = {}, {}, {}, {}, {}, {}
        yh_done, yl_done, routed, score_done = {}, {}, {}, {}
        last = {}

        def A_load(g):
            if g == 0:
                x_loaded[g] = [dma("sync", f"x0_{b}", xr[:, 0, b, :], x_tiles[0][:, b, :]) for b in range(B)]
            else:
                x_loaded[g] = [dma("sync", f"x{g % XR}", xr[:, g % XR, :, :], x_tiles[g], past(xs_stored, g - XR))] * B

        def A_moments(g):
            s, r = g % XR, g % 2
            for b in range(B):
                bn = do("vector", "moments", lambda e, b=b: e.bn_stats(stat[:, b, :], xr[:, s, b, :]),
                        x_loaded[g][b], last.get("aggr"))
            for b in range(B):
                ag = do("vector", "moments", lambda e, b=b: e.bn_aggr(mean_var[:, r, b, :], stat[:, b, :]), bn,
                        past(norm_ready, g - 2))
            last["aggr"] = ag
            moments[g] = ag

        def A_rstd(g):
            r, ag = g % 2, moments[g]
            ve = do("gpsimd", "rstd", lambda e: e.tensor_scalar(
                var_eps[:, :], mean_var[:, r, :, 1], LN_EPS, None, ALU.add), ag, last.get("rstd"))
            do("gpsimd", "rstd", lambda e: e.tensor_scalar(neg_mean[:, :], mean_var[:, r, :, 0], -1.0, None, ALU.mult))
            rs = do("gpsimd", "rstd", lambda e: e.tensor_tensor(
                rstd[:, r, :], var_eps[:, :], minus_half[:, :], ALU.pow), ve, const["all"],
                past(xn_done, g - 2))
            last["rstd"] = norm_ready[g] = do("gpsimd", "rstd", lambda e: e.tensor_tensor(
                shift[:, r, :], neg_mean[:, :], rstd[:, r, :], ALU.mult), rs)

        def A_xn(g):
            s, r = g % XR, g % 2
            xn_batch[g] = []
            for b in range(B):
                xn_done[g] = do("scalar", "xn", lambda e, b=b: e.activation(
                    xn[:, r, b, :], xr[:, s, b, :], ACT.Identity, bias=shift[:, r, b:b + 1], scale=rstd[:, r, b:b + 1]),
                    norm_ready[g], past(y_done, g - 2), past(t_done, g - 2))
                xn_batch[g].append(xn_done[g])

        def A_transpose(g):
            r = g % 2
            wait("tensor", const["ident"], past(xt_done, g - 1))
            for b in range(B):
                wait("tensor", xn_batch[g][b])
                for c in range(KC):
                    f = lambda e, c=c, b=b: e.transpose(
                        tq_ps[:, c, b * P:(b + 1) * P], xn[:, r, b, c * P:(c + 1) * P], ident[:, :])
                    if (c, b) == (KC - 1, B - 1):
                        t_done[g] = do("tensor", "xn_t_ps", f)
                    else:
                        more("tensor", f)

        def A_keep(g):
            r = g % 2
            xt_done[g] = do("scalar", "xn_t", lambda e: e.copy(xt[:, r, :], flat(tq_ps[:, :, :])),
                            t_done[g], past(xt_stored, g - 2), past(xl_done, g - 2))
            xt_stored[g] = dma("sync", f"xts{r}", xt_dram[g], xt[:, r, :], xt_done[g])

        def A_split(g, free):
            r = g % 2
            xh_done[g] = do("scalar", "xh", lambda e: e.copy(xh[:, r, :], xt[:, r, :]), xt_done[g], *free)
            engine = "vector" if g == 0 else "gpsimd"
            xl_done[g] = do(engine, "xl_" + engine, lambda e: e.tensor_tensor(
                xl[:, r, :], xt[:, r, :], xh[:, r, :].bitcast(F32), ALU.subtract), xh_done[g], *free)

        def parts(hi_l, lo_l, hi_r, lo_r):
            return ((hi_l, hi_r), (hi_l, lo_r), (lo_l, hi_r))

        def A_logits(g):
            r = g % 2
            wait("tensor", xh_done[g], xl_done[g], last.get("rps_read"), *router_ready)
            for b in range(B):
                col = b * 2 * RC
                for c in range(KC):
                    tok = slice(c * GT + b * P, c * GT + (b + 1) * P)
                    more("tensor", lambda e, b=b, c=c, tok=tok, col=col: e.matmul(
                        r_ps[:, col:col + 2 * RC], xh[:, r, tok], rw_parts[:, c, :], start=(c == 0), stop=False,
                        skip_group_check=True))
                    f = lambda e, b=b, c=c, tok=tok, col=col: e.matmul(
                        r_ps[:, col:col + RC], xl[:, r, tok], rw_parts[:, c, 0:RC], start=False,
                        stop=(c == KC - 1), skip_group_check=True)
                    if (b, c) == (B - 1, KC - 1):
                        lg_done[g] = do("tensor", "logits_ps", f)
                    else:
                        more("tensor", f)

        def A_logits_out(g):
            lg = logits[:, g % RG, :].rearrange("p (b r) -> p b r", r=RC)
            ps = r_ps[:, 0:B * 2 * RC].rearrange("p (b k r) -> p k b r", k=2, r=RC)
            hi = do("scalar", "logits_hi", lambda e: e.copy(lg, ps[:, 0]),
                    lg_done[g], past(score_done, g // RG - 1), past(y_done, g - RG))
            vs_done[g] = do("vector", "logits", lambda e: e.tensor_tensor(lg, lg, ps[:, 1], ALU.add), hi)
            last["rps_read"] = vs_done[g]

        def A_values(g):
            r = g % 2
            v = lambda b: logits[:, g % RG, b * RC + NE:b * RC + NE + 1]
            t = do("vector", "y", lambda e: e.tensor_scalar(y[:, :], xn[:, r, 0, :], v(0), None, ALU.mult),
                   vs_done[g], past(yt_done, g - 1))
            for b in range(1, B):
                t = do("vector", "y", lambda e, b=b: e.scalar_tensor_tensor(
                    y[:, :], xn[:, r, b, :], v(b), y[:, :], ALU.mult, ALU.add), t)
            y_done[g] = t

        def A_y_transpose(g):
            wait("tensor", y_done[g], last.get("mps_read"))
            for c in range(KC):
                f = lambda e, c=c: e.transpose(m_ps[:, c * P:(c + 1) * P], y[:, c * P:(c + 1) * P], ident[:, :])
                if c == KC - 1:
                    yt_done[g] = do("tensor", "y_t_ps", f)
                else:
                    more("tensor", f)

        def A_y_split(g):
            half = slice((g % SG) * P, (g % SG + 1) * P)
            ps = m_ps[:, 0:D].rearrange("p (c t) -> p c t", c=KC)
            yh_done[g] = do("scalar", "yh", lambda e: e.copy(yh[:, :, half], ps), yt_done[g], last.get("m"))
            yl_done[g] = do("vector", "yl", lambda e: e.tensor_tensor(
                yl[:, :, half], ps, yh[:, :, half].bitcast(F32), ALU.subtract), yh_done[g], last.get("m"))
            last["mps_read"] = yl_done[g]

        def A_scan(g):
            wait("tensor", yh_done[g], yl_done[g], *wk_ready)
            n = SG * P
            for c in range(KC):
                k = 0
                for i in range(KC):
                    col = slice(c * P, (c + 1) * P)
                    for l, w in parts(wk_hi[:, i, col], wk_lo[:, i, col], yh[:, i, :], yl[:, i, :]):
                        f = lambda e, l=l, w=w, c=c, k=k: e.matmul(
                            m_ps[:, c * n:(c + 1) * n], l, w, start=(k == 0), stop=(k == 3 * KC - 1))
                        k += 1
                        if (c, k) == (KC - 1, 3 * KC):
                            last["m"] = do("tensor", "m_ps", f)
                        else:
                            more("tensor", f)
            t0 = (g - SG + 1) * P
            for c in range(KC):
                a = 1 if t0 == 0 else 0
                init = 0.0 if t0 == 0 else state[:, c, t0 - 1:t0]
                s = do("vector", "scan", lambda e, c=c, a=a, init=init: e.tensor_tensor_scan(
                    state[:, c, t0 + a:t0 + n], gamma_col[:, :].broadcast_to([P, n - a]), m_ps[:, c * n + a:(c + 1) * n], init,
                    ALU.mult, ALU.add), last["m"], last.get(f"scan{c}"), const["all"], *staging_free)
                last[f"scan{c}"] = s
            if t0 == 0:
                s = do("vector", "scan", lambda e: e.tensor_copy(state[:, :, 0:1], state[:, :, 1:2]), s)
            last["mps_read"] = last["scan"] = s

        def A_unit(q, s):
            r, w = q % 2, unit_slot(NE + s) * WN
            for name, ps, base, free in (("gate", gate_ps, GATE, last.get("silu")), ("up", up_ps, UP, last.get("hid"))):
                wait("tensor", xh_done[q], xl_done[q], free, *unit_ready[NE + s])
                k = 0
                for c in range(KC):
                    ws = slice(w + base + c * F, w + base + (c + 1) * F)
                    xs = slice(c * GT, (c + 1) * GT)
                    for l, m in parts(w_hi[:, ws], w_lo[:, ws], xh[:, r, xs], xl[:, r, xs]):
                        f = lambda e, l=l, m=m, k=k, ps=ps: e.matmul(ps[:, :], l, m, start=(k == 0), stop=(k == 3 * KC - 1))
                        k += 1
                        if k == 3 * KC:
                            last[name] = do("tensor", name, f)
                        else:
                            more("tensor", f)

        def A_hidden():
            last["silu"] = do("scalar", "silu", lambda e: e.activation(gated[:, :], gate_ps[:, :], ACT.Silu),
                              last["gate"], last.get("hid"))
            last["hid"] = do("vector", "hidden", lambda e: e.tensor_tensor(hid[:, :], gated[:, :], up_ps[:, :], ALU.mult),
                             last["silu"], last["up"], last.get("hh"), last.get("hl"))

        def A_hidden_split(prev_down):
            last["hh"] = do("scalar", "hidden_hi", lambda e: e.copy(hid_hi[:, :], hid[:, :]), last["hid"], prev_down)
            last["hl"] = do("gpsimd", "hidden_lo", lambda e: e.tensor_tensor(
                hid_lo[:, :], hid[:, :], hid_hi[:, :].bitcast(F32), ALU.subtract), last["hh"], prev_down)

        def down_products(e, w, first):
            for b in range(B):
                tok = slice(b * P, (b + 1) * P)
                col = slice(b % 2 * D, (b % 2 + 1) * D)
                for k, (l, m) in enumerate(parts(hid_hi[:, tok], hid_lo[:, tok], w_hi[:, w], w_lo[:, w])):
                    ins = e.matmul(y_ps[:, b // 2, col], l, m, start=(first and b % 2 == 0 and k == 0),
                                   stop=(k == 2), skip_group_check=True)
            return ins

        def A_down(q, s):
            w = unit_slot(NE + s) * WN + DOWN
            last["down"] = do("tensor", "down", lambda e: down_products(e, slice(w, w + D), s == 0),
                              last["hh"], last["hl"], last.get("y_read"))

        def A_add_shared(q):
            xs_added[q] = do("vector", "x_shared", lambda e: e.tensor_tensor(
                xr[:, q % XR, :, :].rearrange("p b d -> p (b d)"),
                xr[:, q % XR, :, :].rearrange("p b d -> p (b d)"), flat(y_ps[:, :, :]), ALU.add),
                last["down"], xn_done[q])
            last["y_read"] = xs_added[q]
            xs_stored[q] = dma("sync", f"xss{q % XR}", xs_dram[q], flat(xr[:, q % XR, :, :]), xs_added[q])

        def A_route(n):
            cols = RT * NE
            lg = logits[:, :, :].rearrange("p g (b r) -> p (g b) r", r=RC)[:, :, 0:NE]
            score_done[n] = do("scalar", "score", lambda e: e.activation(score[:, :, :], lg, ACT.Sigmoid),
                               vs_done[RG * n + RG - 1], *last.get("routed", ()))
            t = score_done[n]
            yield

            def v(f, *tokens):
                return do("vector", "route", f, *tokens)

            sc, sb3 = flat(score[:, :, :]), biased[:, :, :]
            t = v(lambda e: e.tensor_tensor(sb3, score[:, :, :], bias_all[:, :].unsqueeze(1).broadcast_to([P, RT, NE]), ALU.add),
                  t, *last.get("routed", ()), bias_ready)
            yield
            pairs = biased[:, :, :].rearrange("p t (h k) -> p (t h) k", k=2)
            ph, pl = flat(pair_hi[:, :, :]), flat(pair_lo[:, :, :])
            v(lambda e: e.tensor_tensor(ph, pairs[:, :, 0], pairs[:, :, 1], ALU.max), t)
            yield
            t = v(lambda e: e.tensor_tensor(pl, pairs[:, :, 0], pairs[:, :, 1], ALU.min))
            yield
            v(lambda e: e.tensor_tensor(g_a[:, :], pair_hi[:, :, 0], pair_hi[:, :, 1], ALU.min), t)
            yield
            t = v(lambda e: e.tensor_tensor(g_b[:, :], pair_lo[:, :, 0], pair_lo[:, :, 1], ALU.max))
            yield
            t = v(lambda e: e.tensor_tensor(g_a[:, :], g_a[:, :], g_b[:, :], ALU.max), t)
            yield
            t = v(lambda e: e.tensor_tensor(g_b[:, :], pair_hi[:, :, 0], pair_hi[:, :, 1], ALU.max), t)
            yield
            t = v(lambda e: e.tensor_tensor(g_score[:, :], g_a[:, :], g_b[:, :], ALU.add), t)
            yield
            gj = g_score[:, :].rearrange("p (t j) -> p t j", j=EG).unsqueeze(2).broadcast_to([P, RT, EG, EG])
            gi = g_score[:, :].rearrange("p (t i) -> p t i", i=EG).unsqueeze(3).broadcast_to([P, RT, EG, EG])
            ra4 = r_a[:, 0:RT * EG * EG].rearrange("p (t i j) -> p t i j", i=EG, j=EG)
            rb4 = r_b[:, 0:RT * EG * EG].rearrange("p (t i j) -> p t i j", i=EG, j=EG)
            v(lambda e: e.tensor_tensor(ra4, gj, gi, ALU.is_ge), t)
            yield
            t = v(lambda e: e.tensor_tensor(rb4, gj, gi, ALU.is_gt))
            yield
            t = v(lambda e: e.tensor_tensor(ra4, ra4, earlier[:, :, :].unsqueeze(1).broadcast_to([P, RT, EG, EG]), ALU.mult), t, const["all"])
            yield
            t = v(lambda e: e.tensor_tensor(r_a[:, :], r_a[:, :], r_b[:, :], ALU.max), t)
            yield
            t = v(lambda e: e.tensor_reduce(g_a[:, :], r_a[:, :].rearrange("p (t j) -> p t j", j=EG), AX_X, ALU.add), t)
            yield
            t = v(lambda e: e.tensor_scalar(g_a[:, :], g_a[:, :], float(TOP_GROUPS), None, ALU.is_lt), t)
            yield
            masked = r_c[:, :].rearrange("p (t k) -> p t k", k=NE)
            t = v(lambda e: e.tensor_tensor(
                r_c[:, :].rearrange("p (h k) -> p h k", k=EPG), biased[:, :, :].rearrange("p t (h k) -> p (t h) k", k=EPG),
                g_a[:, :].unsqueeze(2).broadcast_to([P, RT * EG, EPG]), ALU.mult), t)
            yield
            for i in range(RT):
                t8 = v(lambda e, i=i: e.max(top8[:, i, :], masked[:, i, :]), t)
                yield
            fourth = top8[:, :, TOP_EXPERTS - 1:TOP_EXPERTS].broadcast_to([P, RT, NE])
            a3 = r_a[:, :].rearrange("p (t k) -> p t k", k=NE)
            b3 = r_b[:, :].rearrange("p (t k) -> p t k", k=NE)
            v(lambda e: e.tensor_tensor(a3, masked, fourth, ALU.is_gt), t8)
            yield
            t = v(lambda e: e.tensor_tensor(b3, masked, fourth, ALU.is_equal))
            yield
            v(lambda e: e.tensor_reduce(t_a[:, :], a3, AX_X, ALU.add), t)
            yield
            t = v(lambda e: e.tensor_tensor_scan(r_c[:, :], flat(restart[:, :, :]), r_b[:, :], 0.0, ALU.mult, ALU.add), t)
            yield
            t = v(lambda e: e.tensor_tensor(masked, masked, t_a[:, :].unsqueeze(2).broadcast_to([P, RT, NE]), ALU.add), t)
            yield
            t = v(lambda e: e.scalar_tensor_tensor(r_c[:, :], r_c[:, :], float(TOP_EXPERTS), r_b[:, :], ALU.is_le, ALU.mult), t)
            yield
            t = v(lambda e: e.tensor_tensor(flat(chosen[:, :, :]), r_a[:, :], r_c[:, :], ALU.add), t)
            yield
            last["chosen16"] = do("gpsimd", "chosen16", lambda e: e.tensor_copy(chosen16[:, :], flat(chosen[:, :, :])),
                                  t, last.get("count"))
            yield
            t = v(lambda e: e.tensor_tensor(r_a[:, :], sc, flat(chosen[:, :, :]), ALU.mult), t)
            yield
            t = v(lambda e: e.tensor_reduce(t_a[:, :], a3, AX_X, ALU.add), t)
            yield
            t = v(lambda e: e.tensor_scalar(t_a[:, :], t_a[:, :], 1e-20, None, ALU.add), t)
            yield
            t = v(lambda e: e.reciprocal(t_a[:, :], t_a[:, :]), t)
            yield
            t = v(lambda e: e.scalar_tensor_tensor(a3, a3, ROUTE_SCALE, t_a[:, :].unsqueeze(2).broadcast_to([P, RT, NE]), ALU.mult, ALU.mult), t)
            yield
            part = lambda k: combine16[:, n * RT:(n + 1) * RT, k * NE:(k + 1) * NE]
            p = t
            for f in (lambda e: e.tensor_copy(part(0), a3),
                      lambda e: e.tensor_tensor(a3, a3, part(0), ALU.subtract),
                      lambda e: e.tensor_copy(part(1), a3),
                      lambda e: e.tensor_tensor(part(2), a3, part(1), ALU.subtract)):
                p = do("gpsimd", "part", f, p)
                yield
            count = r_ps[0:1, 0:cols]
            last["count"] = do("tensor", "count", lambda e: e.matmul(count, ones16[:, 0:1], chosen16[:, :], start=True, stop=True),
                               last["chosen16"], last.get("rps_read"), const["all"])
            last["rps_read"] = t = v(lambda e: e.tensor_reduce(
                r_b[0:1, 0:RG * NE].rearrange("p (g k) -> p g k", k=NE),
                count.rearrange("p (g b k) -> p g k b", b=B, k=NE), AX_X, ALU.add), last["count"], t)
            yield
            t = v(lambda e: e.tensor_copy(counts[0:1, n * RG * NE:(n + 1) * RG * NE], r_b[0:1, 0:RG * NE]), t)
            last["routed"] = routed[n] = [t, p]

        xt_loaded, xs_loaded, bh, bl, ct_ps, ct_done, q_done = {}, {}, {}, {}, {}, {}, {}
        sq_done, sq_added, y_added, stored, cleared = {}, {}, {}, {}, {}

        def B_load(g):
            xt_loaded[g] = dma("sync", f"bxt{g % 2}", xt[:, g % 2, :], xt_dram[g], xt_stored[g],
                               *([bh[g - 2], bl[g - 2]] if g >= 2 else
                                 [xt_stored[NG - 2 + g], xh_done[NG - 2 + g], xl_done[NG - 2 + g]]))
            xs_loaded[g] = dma("sync", f"bx{g % XR}", flat(xr[:, g % XR, :, :]), xs_dram[g], xs_stored[g],
                               *([stored[g - XR]] if g >= XR else [xs_stored[NG - XR + g]]),
                               *(unit_ready[NE - 1] if g == SPARE else []))

        def B_split(g):
            free = [q_done[g - 1]] if g >= 2 else [units_done[NG - 2 + g], lg_done[NG - 2 + g]]
            bh[g] = do("scalar", "b_xh", lambda e: e.copy(xh[:, g % 2, :], xt[:, g % 2, :]), xt_loaded[g], *free)
            bl[g] = do("gpsimd", "b_xl", lambda e: e.tensor_tensor(
                xl[:, g % 2, :], xt[:, g % 2, :], xh[:, g % 2, :].bitcast(F32), ALU.subtract), bh[g], *free)

        def B_combine(g):
            wait("tensor", last["rps_read"], *routed[g // RG], const["ident16"])
            for b in range(B):
                f = lambda e, b=b: e.matmul(r_ps[0:3 * NE, b * P:(b + 1) * P], combine16[:, g * B + b, :],
                                            ident16[:, :], start=True, stop=True)
                if b == B - 1:
                    ct_ps[g] = do("tensor", "combine_t_ps", f)
                else:
                    more("tensor", f)
            ct_done[g] = do("scalar", "combine_t", lambda e: e.copy(ct[:, g % 2, :], r_ps[0:3 * NE, :]), ct_ps[g], past(q_done, g - 1))
            last["rps_read"] = ct_done[g]

        def B_query(g):
            wait("tensor", bh[g], bl[g], sq_done[g - 1] if g > 0 else xt_done[NG - 1], *wq_ready)
            for b in range(B):
                for c in range(KC):
                    tok = slice(c * GT + b * P, c * GT + (b + 1) * P)
                    for k, (l, w) in enumerate(parts(xh[:, g % 2, tok], xl[:, g % 2, tok], wq_hi[:, c, :], wq_lo[:, c, :])):
                        f = lambda e, l=l, w=w, b=b, c=c, k=k: e.matmul(
                            tq_ps[:, b // 2, b % 2 * D:(b % 2 + 1) * D], l, w, start=(c == 0 and k == 0),
                            stop=(c == KC - 1 and k == 2))
                        if (b, c, k) == (B - 1, KC - 1, 2):
                            q_done[g] = do("tensor", "q_ps", f)
                        else:
                            more("tensor", f)

        def new_sem(name):
            return ctx.enter_context(nc.semaphore(name))

        cb_s, gate_s, up_s, silu_s, comb_s, hid_s, hh_s, hl_s, down_hi_s, down_s = (
            new_sem("u_" + n) for n in ("combine_ps", "gate", "up", "silu", "weighted", "hid", "hh", "hl", "down_hi", "down"))
        ENG = ("tensor", "scalar", "vector")
        regs = {e: {} for e in ENG}
        raised_by = {"tensor": (cb_s, gate_s, up_s, down_hi_s, down_s), "scalar": (silu_s,), "vector": (comb_s, hh_s, hid_s, hl_s)}

        def start(name):
            def f(e):
                r = regs[name]
                r["count"] = [e.alloc_register(f"{name}_c{i}") for i in range(NE)]
                r["some"] = [e.alloc_register(f"{name}_h{i}") for i in range(EG)]
                for k in ("done", "next") + (("prev", "have") if name == "tensor" else ()):
                    r[k] = e.alloc_register(f"{name}_{k}")
                e.reg_mov(r["done"], 1)
                e.reg_mov(r["next"], 2)
                if name == "tensor":
                    e.reg_mov(r["prev"], DOWN)
                for s in raised_by[name]:
                    e.sem_inc(s, 1)
            return f

        for n in ENG:
            prog.raw(n, start(n))

        A_load(0)
        rows = lambda w: w.rearrange("(c p) n -> p c n", p=P)
        rw_loaded = dma("sync", "rw", rw[:, :, 0:NE], rows(router))
        bias_ready = dma("sync", "bias", bias_all[:, :], bias.unsqueeze(0).broadcast_to([P, NE]))
        chunks = lambda a: a.rearrange("p (c n) -> p c n", c=KC)
        wv_raw = stage(KC * D)
        wv_loaded = dma("sync", "wv", chunks(wv_raw), rows(wv))
        shared_raw = [stage(WN) for _ in range(NSH)]
        shared_landed = [dma("sync", f"unit{i}", raw, experts[NE + i]) for i, raw in enumerate(shared_raw)]
        A_load(1)
        wk_raw, wq_raw = stage(KC * D), stage(KC * D)
        wk_landed = dma("sync", "wk", chunks(wk_raw), rows(wk))
        wq_landed = dma("sync", "wq", chunks(wq_raw), rows(wq))
        A_moments(0)
        A_rstd(0)
        do("vector", "router_sums", lambda e: e.memset(rw[:, :, NE + 1:RC], 0.0))
        rs = do("vector", "router_sums", lambda e: e.tensor_reduce(rw[:, :, NE:NE + 1], chunks(wv_raw), AX_X, ALU.add), wv_loaded)
        rh = do("scalar", "router_hi", lambda e: e.copy(rw_parts[:, :, 0:RC], rw[:, :, :]), rw_loaded, rs)
        A_xn(0)
        A_moments(1)
        A_rstd(1)
        rl = do("vector", "router_lo", lambda e: e.tensor_tensor(
            rw_parts[:, :, RC:2 * RC], rw[:, :, :], rw_parts[:, :, 0:RC].bitcast(F32), ALU.subtract), rw_loaded, rs, rh)
        router_ready = [rh, rl]

        def split_first_weights():
            for i in range(NSH):
                split_unit(NE + i, shared_landed[i], shared_raw[i], engine="vector")
            k = split(wk_landed, wk_raw, flat(wk_hi[:, :, :]), flat(wk_lo[:, :, :]), engine="vector")
            q = split(wq_landed, wq_raw, flat(wq_hi[:, :, :]), flat(wq_lo[:, :, :]), engine="vector")
            return k, q

        early_units = NE - NSH
        SPARE = 2
        ROUTE_STEPS = (10, 4)
        route_steps = []

        def route(steps):
            for _ in range(steps):
                if route_steps and next(route_steps[0], "end") == "end":
                    route_steps.pop(0)

        units_done, unit_landed = {}, {}
        for g in range(NG + 2):
            if g <= early_units:
                unit_landed[g] = dma("sync", "w_raw", w_raw[:, :], experts[g], *unit_ready.get(g - 1, ()))
            q = g - 1
            if g < NG:
                A_transpose(g)
                A_keep(g)
            if 0 <= q < NG:
                A_unit(q, 0)
            if g < NG:
                A_split(g, [past(units_done, g - 2), past(lg_done, g - 2)])
            elif g == NG:
                B_load(0)
                B_load(1)
                B_split(0)
            if g == 0:
                wk_ready, wq_ready = split_first_weights()
                staging_free = [rs] + unit_ready[NE] + unit_ready[NU - 1] + wk_ready + wq_ready
            if 0 <= q < NG:
                A_hidden()
            if 1 <= q <= NG:
                A_down(q - 1, 1)
            if 0 <= q < NG:
                A_y_transpose(q)
            if 0 < g and g + 1 < NG:
                A_moments(g + 1)
            if 0 <= q < NG:
                A_hidden_split(last.get("down"))
                A_y_split(q)
            if 1 <= q <= NG:
                A_add_shared(q - 1)
            if g + 2 < NG:
                A_load(g + 2)
            if 0 < g and g + 1 < NG:
                A_rstd(g + 1)
            if g <= NG:
                route(ROUTE_STEPS[0])
            if g < early_units:
                split_unit(g, unit_landed[g], w_raw[:, :])
            if 0 <= q < NG:
                A_unit(q, 1)
                units_done[q] = last["up"]
                A_hidden()
                if q % SG == SG - 1:
                    A_scan(q)
            if g + 1 < NG:
                A_xn(g + 1)
            if 0 <= q < NG:
                A_down(q, 0)
                A_hidden_split(last["down"])
            if g <= NG:
                route(ROUTE_STEPS[1])
            if g < NG:
                A_logits(g)
                A_logits_out(g)
                A_values(g)
                if g % RG == RG - 1:
                    route_steps.append(A_route(g // RG))
            elif g == NG:
                B_combine(0)
                B_query(0)
        spare = flat(xr[:, SPARE, :, :])[:, 0:WN]
        last_landed = dma("sync", "w_last", spare, experts[NE - 1], xs_stored[NG - XR + SPARE])

        wait("tensor", last["silu"], last["hid"], last["mps_read"])
        wait("tensor", *unit_ready[early_units - 1])
        wait("scalar", last["hid"], last["down"], last["hl"])
        wait("vector", last["hh"], last["hl"], last["down"], last["scan"], y_done[NG - 1], t_done[NG - 1])

        def begin_units(g):
            for name in ENG:
                wait(name, *routed[g // RG])

                def f(e, r=regs[name]):
                    e.load(r["count"], counts[0:1, g * NE:(g + 1) * NE])
                    for h in range(EG):
                        first, *others = r["count"][h * EPG:(h + 1) * EPG]
                        e.reg_mov(r["some"][h], first)
                        for c in others:
                            e.reg_add(r["some"][h], r["some"][h], c)
                prog.raw(name, f)
            prog.raw("tensor", lambda e: e.reg_mov(regs["tensor"]["have"], 0))

        def units(g, h):
            for name, body in (("tensor", tensor_unit), ("scalar", scalar_unit), ("vector", vector_unit)):
                def f(e, r=regs[name], body=body):
                    with e.If_ne(r["some"][h], 0):
                        for u in range(h * EPG, (h + 1) * EPG):
                            with e.If_ne(r["count"][u], 0):
                                body(e, r, g, u, e.snap(r["done"]), e.snap(r["next"]))
                                e.reg_add(r["done"], r["done"], 1)
                                e.reg_add(r["next"], r["next"], 1)
                prog.raw(name, f)

        def B_attend(g):
            t0 = g * P
            s = state[:, (t0 % D) // P, t0 // D::T // D].unsqueeze(1).broadcast_to([P, B, D])
            q = flat(tq_ps[:, :, :]).rearrange("p (b d) -> p b d", b=B)
            sq_done[g] = do("vector", "state_q", lambda e: e.tensor_tensor(sq, q, s, ALU.mult), q_done[g], past(sq_added, g - 1))
            xg = flat(xr[:, g % XR, :, :])
            sq_added[g] = do("gpsimd", "attended", lambda e: e.tensor_tensor(xg, xg, flat(sq), ALU.add), sq_done[g], xs_loaded[g])

        def B_finish(g):
            prog.raw("vector", lambda e: e.wait_ge(down_s, e.snap(regs["vector"]["done"])))
            xg = flat(xr[:, g % XR, :, :])
            y_added[g] = do("vector", "out_ready", lambda e: e.tensor_tensor(xg, xg, flat(y_ps[:, :, :]), ALU.add),
                            sq_added[g])
            stored[g] = dma("sync", f"out{g % XR}", out_tiles[g], xr[:, g % XR, :, :], y_added[g])

        def B_clear(g):
            cleared[g] = do("vector", "clear", lambda e: e.memset(flat(y_ps[:, :, :]), 0.0),
                            past(y_added, g - 1), last["y_read"])

        def down_dynamic(e, r, g):
            at = e.snap(r["prev"], min_val=DOWN, max_val=(NE - 1) * WN + DOWN)

            def products(hid_part, down_parts):
                for b in range(B):
                    for w in down_parts:
                        ins = e.matmul(y_ps[:, b // 2, b % 2 * D:(b % 2 + 1) * D], hid_part[:, b * P:(b + 1) * P],
                                       w[:, bass.ds(at, D)], start=False, stop=True, skip_group_check=True)
                return ins

            def high(done):
                e.wait_ge(prog.sem(cleared[g][0])[0], cleared[g][1])
                e.wait_ge(hh_s, done)
                products(hid_hi, (w_hi, w_lo)).then_inc(down_hi_s, 1)

            def low(done):
                e.wait_ge(hl_s, done)
                products(hid_lo, (w_hi,)).then_inc(down_s, 1)

            return high, low

        def tensor_unit(e, r, g, u, done, nxt):
            if g == 0 and u >= early_units:
                for sem_name, value in unit_ready[u]:
                    e.wait_ge(prog.sem(sem_name)[0], value)
            w = u * WN

            def inward(ps, base, sem):
                k = 0
                for c in range(KC):
                    ws = slice(w + base + c * F, w + base + (c + 1) * F)
                    xs = slice(c * GT, (c + 1) * GT)
                    for l, m in parts(w_hi[:, ws], w_lo[:, ws], xh[:, g % 2, xs], xl[:, g % 2, xs]):
                        ins = e.matmul(ps[:, :], l, m, start=(k == 0), stop=(k == 3 * KC - 1))
                        k += 1
                ins.then_inc(sem, 1)

            def combine_weights():
                e.wait_ge(comb_s, done)
                e.matmul(m_ps[:, :], pick[:, u:u + 1].broadcast_to([3 * NE, P]), ct[:, g % 2, :],
                         start=True, stop=True).then_inc(cb_s, 1)

            def gate():
                e.wait_ge(silu_s, done)
                inward(gate_ps, GATE, gate_s)

            def up():
                e.wait_ge(hid_s, done)
                inward(up_ps, UP, up_s)

            gate()
            with e.If_ne(r["have"], 0):
                down_high, down_low = down_dynamic(e, r, g)
                down_high(done)
                combine_weights()
                up()
                down_low(done)
            with e.Else():
                combine_weights()
                up()
            e.reg_mov(r["have"], 1)
            e.reg_mov(r["prev"], w + DOWN)

        def B_flush(g):
            def f(e):
                r = regs["tensor"]
                done = e.snap(r["done"])
                down_high, down_low = down_dynamic(e, r, g)
                down_high(done)
                down_low(done)
            prog.raw("tensor", f)

        def scalar_unit(e, r, g, u, done, nxt):
            e.wait_ge(gate_s, nxt)
            e.wait_ge(hid_s, done)
            e.activation(gated[:, :], gate_ps[:, :], ACT.Silu).then_inc(silu_s, 1)

        def vector_unit(e, r, g, u, done, nxt):
            e.wait_ge(silu_s, nxt)
            e.wait_ge(cb_s, nxt)
            e.tensor_tensor(gated[:, :], gated[:, :], m_ps[:, :], ALU.mult).then_inc(comb_s, 1)
            e.wait_ge(comb_s, nxt)
            e.wait_ge(up_s, nxt)
            e.wait_ge(down_hi_s, done)
            e.tensor_tensor(hid_hi[:, :], gated[:, :], up_ps[:, :], ALU.mult).then_inc(hh_s, 1)
            e.wait_ge(hl_s, done)
            e.tensor_tensor(hid[:, :], gated[:, :], up_ps[:, :], ALU.mult).then_inc(hid_s, 1)
            e.wait_ge(hh_s, nxt)
            e.wait_ge(hid_s, nxt)
            e.wait_ge(down_s, done)
            e.tensor_tensor(hid_lo[:, :], hid[:, :], hid_hi[:, :].bitcast(F32), ALU.subtract).then_inc(hl_s, 1)

        for g in range(NG):
            wait("tensor", bh[g], bl[g], ct_done[g])
            if g == 1:
                wait("tensor", *unit_ready[early_units], *unit_ready[NE - 1])
            B_attend(g)
            if g > 0:
                B_finish(g - 1)
            B_clear(g)
            if g + 1 < NG:
                B_split(g + 1)
            begin_units(g)
            for h in range(EG):
                units(g, h)
                if g < NG - RG:
                    route(2)
                if (g, h) == (0, 0):
                    split_unit(early_units, unit_landed[early_units], w_raw[:, :], [last["down"]])
                    split_unit(NE - 1, last_landed, spare, [last["down"]])
            if g + 2 < NG:
                B_load(g + 2)
            if g + 1 < NG:
                B_combine(g + 1)
                B_query(g + 1)
            B_flush(g)
        B_finish(NG - 1)
        wait("sync", *[stored[g] for g in range(NG - XR, NG)])

        block = ctx.enter_context(nc.Block())

        @block.sync
        def _(e):
            prog.run("sync", e)

        @block.scalar
        def _(e):
            prog.run("scalar", e)

        @block.vector
        def _(e):
            prog.run("vector", e)

        @block.gpsimd
        def _(e):
            prog.run("gpsimd", e)

        @block.tensor
        def _(e):
            prog.run("tensor", e)


def kernel(L0_attn_x, L0_attn_Wq, L0_attn_Wk, L0_attn_Wv, L0_ffn_router_weight, L0_ffn_e_bias, L0_ffn_gate_w,
           L0_ffn_up_w, L0_ffn_down_w, L0_ffn_sh_gate_w, L0_ffn_sh_up_w, L0_ffn_sh_down_w):
    import numpy as np
    import concourse.bacc as bacc
    from concourse.bass_utils import run_bass_kernel_spmd

    x = np.ascontiguousarray(L0_attn_x)
    D = x.shape[-1]
    E, F, _ = L0_ffn_gate_w.shape
    NSH = L0_ffn_sh_gate_w.shape[0] // F
    KC = D // P

    def inward(w):
        w = np.asarray(w)
        return w.reshape(w.shape[0], F, KC, P).transpose(0, 3, 2, 1).reshape(w.shape[0], P, KC * F)

    def outward(w):
        return np.asarray(w).transpose(0, 2, 1)

    gate = np.concatenate([inward(L0_ffn_gate_w), inward(np.asarray(L0_ffn_sh_gate_w).reshape(NSH, F, D))])
    up = np.concatenate([inward(L0_ffn_up_w), inward(np.asarray(L0_ffn_sh_up_w).reshape(NSH, F, D))])
    sh_down = np.asarray(L0_ffn_sh_down_w).reshape(D, NSH, F).transpose(1, 0, 2)
    down = np.concatenate([outward(L0_ffn_down_w), outward(sh_down)])
    arrays = {
        "x": x,
        "wq": np.ascontiguousarray(L0_attn_Wq),
        "wk": np.ascontiguousarray(L0_attn_Wk),
        "wv": np.ascontiguousarray(L0_attn_Wv),
        "router": np.ascontiguousarray(np.asarray(L0_ffn_router_weight).T),
        "bias": np.ascontiguousarray(L0_ffn_e_bias),
        "experts": np.ascontiguousarray(np.concatenate([gate, up, down], axis=2)),
    }
    nc = bacc.Bacc("TRN2", target_bir_lowering=False, num_devices=1)
    args = [nc.dram_tensor(n, a.shape, mybir.dt.from_np(a.dtype), kind="ExternalInput").ap() for n, a in arrays.items()]
    out = nc.dram_tensor("out", x.shape, F32, kind="ExternalOutput").ap()
    layer_kernel(nc, *args, out)
    r = run_bass_kernel_spmd(nc, [arrays], core_ids=[0])
    return r.results[0]["out"]
```
